# Optimizing a Trainium2 kernel written in Bass

```python
import numpy as np
import jax
import jax.numpy as jnp

def _softmax(x, axis=-1):
    return jax.nn.softmax(x, axis=axis)

def _gelu(x):
    return jax.nn.gelu(x, approximate=True)

def _silu(x):
    return jax.nn.silu(x)

def _sigmoid(x):
    return jax.nn.sigmoid(x)

def _layernorm(x, axis=-1, eps=1e-05):
    m = jnp.mean(x, axis=axis, keepdims=True)
    v = jnp.var(x, axis=axis, keepdims=True)
    return (x - m) / jnp.sqrt(v + eps)

def _scatter_add(tgt, idx, src, axis=0):
    return tgt.at[idx].add(src)

def _segment_sum(src, seg, n):
    return jax.ops.segment_sum(src, seg, n)
kernel_name = 'mk_recurrent_d1_jaxref_r4_43605a'

def setup_inputs(seed: int=0):
    np.random.seed(seed)
    _w = jnp.asarray

    def _L0_attn_setup():
        import jax, jax.numpy as jnp
        import numpy as np
        from jax import lax
        B, T, C = (4, 256, 256)
        N = 64
        H = C // N
        D_MIX, D_DECAY, D_LORA, D_GATE = (32, 64, 16, 128)
        EPS = 0.00064

        def wkv7(r, w, k, v, a, b):
            B_, T_, C_ = r.shape
            resh = lambda t: t.reshape(B_, T_, H, N).transpose(1, 0, 2, 3)
            rT, kT, vT, aT, bT = map(resh, (r, k, v, a, b))
            dT = jnp.exp(resh(w))

            def step(S, inp):
                rt, dt, kt, vt, at, bt = inp
                sa = jnp.einsum('bhij,bhj->bhi', S, at)
                S = S * dt[:, :, None, :] + sa[..., None] * bt[:, :, None, :] + vt[..., None] * kt[:, :, None, :]
                y = jnp.einsum('bhij,bhj->bhi', S, rt)
                return (S, y)
            S0 = jnp.zeros((B_, H, N, N), r.dtype)
            _, ys = lax.scan(step, S0, (rT, dT, kT, vT, aT, bT))
            return ys.transpose(1, 0, 2, 3).reshape(B_, T_, C_)

        def _forward(x, time_maa_x, time_maa_rg, time_maa_wa, time_maa_k, time_maa_v, time_maa_w1, time_maa_w2, time_decay, time_decay_w1, time_decay_w2, time_faaaa, time_aaaaa, time_aaa_w1, time_aaa_w2, time_kkk_w1, time_kkk_w2, gate_w1, gate_w2, ma_w1, ma_w2, time_misc_a, mk_w1, mk_w2, time_misc_k, w_receptance, w_key, w_value, w_output, ln_w, ln_b):
            B_, T_, C_ = x.shape
            xprev = jnp.concatenate([jnp.zeros_like(x[:, :1]), x[:, :-1]], axis=1)
            xx = xprev - x
            mix_in = jnp.tanh((x + xx * time_maa_x) @ time_maa_w1)
            mix = jnp.einsum('btfd,fdc->fbtc', mix_in.reshape(B_, T_, 4, D_MIX), time_maa_w2)
            mrg, mwa, mk_, mv_ = (mix[0], mix[1], mix[2], mix[3])
            xrg = x + xx * (time_maa_rg + mrg)
            xwa = x + xx * (time_maa_wa + mwa)
            xk = x + xx * (time_maa_k + mk_)
            xv = x + xx * (time_maa_v + mv_)
            r = xrg @ w_receptance.T
            w = -jax.nn.softplus(-(time_decay + jnp.tanh(xwa @ time_decay_w1) @ time_decay_w2)) - 0.5
            k = xk @ w_key.T
            v = xv @ w_value.T
            g = jnp.tanh(xrg @ gate_w1) @ gate_w2
            kk = k + jnp.tanh(xk @ time_kkk_w1) @ time_kkk_w2
            kk4 = kk.reshape(B_, T_, H, N)
            kk4 = kk4 / jnp.maximum(jnp.linalg.norm(kk4, axis=-1, keepdims=True), 1e-12)
            kk = kk4.reshape(B_, T_, C_)
            a = jax.nn.sigmoid(time_aaaaa + xwa @ time_aaa_w1 @ time_aaa_w2)
            ma = jax.nn.sigmoid(time_misc_a + xwa @ ma_w1 @ ma_w2)
            k = k * ma + k * a * (1.0 - ma)
            mk2 = jax.nn.sigmoid(time_misc_k + xk @ mk_w1 @ mk_w2)
            k = k * jnp.exp(jnp.minimum(w * mk2, 0.0))
            y = wkv7(r, w, k, v, -kk, kk * a)
            yh = y.reshape(B_ * T_, H, N)
            mu = yh.mean(-1, keepdims=True)
            var = yh.var(-1, keepdims=True)
            yh = (yh - mu) * lax.rsqrt(var + EPS)
            y = (yh.reshape(B_ * T_, C_) * ln_w + ln_b).reshape(B_, T_, C_)
            rr = r.reshape(B_, T_, H, N)
            kr = k.reshape(B_, T_, H, N)
            vr = v.reshape(B_, T_, H, N)
            y = y + ((rr * kr * time_faaaa).sum(-1, keepdims=True) * vr).reshape(B_, T_, C_)
            return y * g @ w_output.T
        key = jax.random.key(seed)
        ks = iter(jax.random.split(key, 48))
        rn = lambda shape, s=1.0: jax.random.normal(next(ks), shape, dtype=jnp.float32) * s
        un = lambda shape, lo, hi: jax.random.uniform(next(ks), shape, minval=lo, maxval=hi, dtype=jnp.float32)
        p = {'x': rn((B, T, C))}
        for nm in ('time_maa_x', 'time_maa_rg', 'time_maa_wa', 'time_maa_k', 'time_maa_v'):
            p[nm] = un((1, 1, C), 0.0, 1.0)
        p['time_maa_w1'] = rn((C, 4 * D_MIX), 0.01)
        p['time_maa_w2'] = rn((4, D_MIX, C), 0.05)
        p['time_decay'] = un((1, 1, C), -6.5, -1.0) + 0.5
        p['time_decay_w1'] = rn((C, D_DECAY), 0.01)
        p['time_decay_w2'] = rn((D_DECAY, C), 0.05)
        p['time_faaaa'] = rn((1, 1, H, N), 0.1)
        p['time_aaaaa'] = jnp.zeros((1, 1, C), jnp.float32)
        p['time_aaa_w1'] = rn((C, D_LORA), 0.01)
        p['time_aaa_w2'] = rn((D_LORA, C), 0.05)
        p['time_kkk_w1'] = rn((C, D_LORA), 0.01)
        p['time_kkk_w2'] = rn((D_LORA, C), 0.05)
        p['gate_w1'] = rn((C, D_GATE), 0.05)
        p['gate_w2'] = rn((D_GATE, C), 0.05)
        p['ma_w1'] = rn((C, D_LORA), 0.01)
        p['ma_w2'] = rn((D_LORA, C), 0.05)
        p['time_misc_a'] = jnp.zeros((1, 1, C), jnp.float32)
        p['mk_w1'] = rn((C, D_LORA), 0.01)
        p['mk_w2'] = rn((D_LORA, C), 0.05)
        p['time_misc_k'] = jnp.zeros((1, 1, C), jnp.float32)
        s = 0.5 / C ** 0.5
        p['w_receptance'] = un((C, C), -s, s)
        p['w_key'] = un((C, C), -0.1 * s, 0.1 * s)
        p['w_value'] = un((C, C), -s, s)
        p['w_output'] = rn((C, C), 0.02)
        p['ln_w'] = jnp.ones((C,), jnp.float32)
        p['ln_b'] = jnp.zeros((C,), jnp.float32)
        return p
    _L0_attn_in = _L0_attn_setup()

    def _L0_ffn_setup():
        import jax, jax.numpy as jnp
        import numpy as np
        DIM = 256
        HIDDEN = 768
        SCALE = 1.0 / 127.0

        def _dequant(w_int, dtype):
            return w_int.astype(dtype) * jnp.asarray(SCALE, dtype)
        key = jax.random.key(seed)
        k_x, k_g, k_u, k_d = jax.random.split(key, 4)
        x = jax.random.normal(k_x, (4, 512, DIM), dtype=jnp.float32)
        w_gate = jax.random.randint(k_g, (HIDDEN, DIM), -127, 128, dtype=jnp.int32)
        w_up = jax.random.randint(k_u, (HIDDEN, DIM), -127, 128, dtype=jnp.int32)
        w_down = jax.random.randint(k_d, (DIM, HIDDEN), -127, 128, dtype=jnp.int32)
        return {'x': x, 'w_gate': w_gate, 'w_up': w_up, 'w_down': w_down}
    _L0_ffn_in = _L0_ffn_setup()
    _d = {'L0_attn_x': _L0_attn_in['x'], 'L0_attn_time_maa_x': _L0_attn_in['time_maa_x'], 'L0_attn_time_maa_rg': _L0_attn_in['time_maa_rg'], 'L0_attn_time_maa_wa': _L0_attn_in['time_maa_wa'], 'L0_attn_time_maa_k': _L0_attn_in['time_maa_k'], 'L0_attn_time_maa_v': _L0_attn_in['time_maa_v'], 'L0_attn_time_maa_w1': _L0_attn_in['time_maa_w1'], 'L0_attn_time_maa_w2': _L0_attn_in['time_maa_w2'], 'L0_attn_time_decay': _L0_attn_in['time_decay'], 'L0_attn_time_decay_w1': _L0_attn_in['time_decay_w1'], 'L0_attn_time_decay_w2': _L0_attn_in['time_decay_w2'], 'L0_attn_time_faaaa': _L0_attn_in['time_faaaa'], 'L0_attn_time_aaaaa': _L0_attn_in['time_aaaaa'], 'L0_attn_time_aaa_w1': _L0_attn_in['time_aaa_w1'], 'L0_attn_time_aaa_w2': _L0_attn_in['time_aaa_w2'], 'L0_attn_time_kkk_w1': _L0_attn_in['time_kkk_w1'], 'L0_attn_time_kkk_w2': _L0_attn_in['time_kkk_w2'], 'L0_attn_gate_w1': _L0_attn_in['gate_w1'], 'L0_attn_gate_w2': _L0_attn_in['gate_w2'], 'L0_attn_ma_w1': _L0_attn_in['ma_w1'], 'L0_attn_ma_w2': _L0_attn_in['ma_w2'], 'L0_attn_time_misc_a': _L0_attn_in['time_misc_a'], 'L0_attn_mk_w1': _L0_attn_in['mk_w1'], 'L0_attn_mk_w2': _L0_attn_in['mk_w2'], 'L0_attn_time_misc_k': _L0_attn_in['time_misc_k'], 'L0_attn_w_receptance': _L0_attn_in['w_receptance'], 'L0_attn_w_key': _L0_attn_in['w_key'], 'L0_attn_w_value': _L0_attn_in['w_value'], 'L0_attn_w_output': _L0_attn_in['w_output'], 'L0_attn_ln_w': _L0_attn_in['ln_w'], 'L0_attn_ln_b': _L0_attn_in['ln_b'], 'L0_ffn_w_gate': _L0_ffn_in['w_gate'], 'L0_ffn_w_up': _L0_ffn_in['w_up'], 'L0_ffn_w_down': _L0_ffn_in['w_down']}
    _x0 = _d['L0_attn_x']
    _d['L0_attn_x'] = jax.random.normal(jax.random.fold_in(jax.random.key(seed), 1), (2, 4096, 256), dtype=_x0.dtype)
    del _x0
    return _d

def reference(L0_attn_x, L0_attn_time_maa_x, L0_attn_time_maa_rg, L0_attn_time_maa_wa, L0_attn_time_maa_k, L0_attn_time_maa_v, L0_attn_time_maa_w1, L0_attn_time_maa_w2, L0_attn_time_decay, L0_attn_time_decay_w1, L0_attn_time_decay_w2, L0_attn_time_faaaa, L0_attn_time_aaaaa, L0_attn_time_aaa_w1, L0_attn_time_aaa_w2, L0_attn_time_kkk_w1, L0_attn_time_kkk_w2, L0_attn_gate_w1, L0_attn_gate_w2, L0_attn_ma_w1, L0_attn_ma_w2, L0_attn_time_misc_a, L0_attn_mk_w1, L0_attn_mk_w2, L0_attn_time_misc_k, L0_attn_w_receptance, L0_attn_w_key, L0_attn_w_value, L0_attn_w_output, L0_attn_ln_w, L0_attn_ln_b, L0_ffn_w_gate, L0_ffn_w_up, L0_ffn_w_down):

    def _L0_attn_ref(x, time_maa_x, time_maa_rg, time_maa_wa, time_maa_k, time_maa_v, time_maa_w1, time_maa_w2, time_decay, time_decay_w1, time_decay_w2, time_faaaa, time_aaaaa, time_aaa_w1, time_aaa_w2, time_kkk_w1, time_kkk_w2, gate_w1, gate_w2, ma_w1, ma_w2, time_misc_a, mk_w1, mk_w2, time_misc_k, w_receptance, w_key, w_value, w_output, ln_w, ln_b):
        import jax, jax.numpy as jnp
        import numpy as np
        from jax import lax
        B, T, C = (4, 256, 256)
        N = 64
        H = C // N
        D_MIX, D_DECAY, D_LORA, D_GATE = (32, 64, 16, 128)
        EPS = 0.00064

        def wkv7(r, w, k, v, a, b):
            B_, T_, C_ = r.shape
            resh = lambda t: t.reshape(B_, T_, H, N).transpose(1, 0, 2, 3)
            rT, kT, vT, aT, bT = map(resh, (r, k, v, a, b))
            dT = jnp.exp(resh(w))

            def step(S, inp):
                rt, dt, kt, vt, at, bt = inp
                sa = jnp.einsum('bhij,bhj->bhi', S, at)
                S = S * dt[:, :, None, :] + sa[..., None] * bt[:, :, None, :] + vt[..., None] * kt[:, :, None, :]
                y = jnp.einsum('bhij,bhj->bhi', S, rt)
                return (S, y)
            S0 = jnp.zeros((B_, H, N, N), r.dtype)
            _, ys = lax.scan(step, S0, (rT, dT, kT, vT, aT, bT))
            return ys.transpose(1, 0, 2, 3).reshape(B_, T_, C_)

        def _forward(x, time_maa_x, time_maa_rg, time_maa_wa, time_maa_k, time_maa_v, time_maa_w1, time_maa_w2, time_decay, time_decay_w1, time_decay_w2, time_faaaa, time_aaaaa, time_aaa_w1, time_aaa_w2, time_kkk_w1, time_kkk_w2, gate_w1, gate_w2, ma_w1, ma_w2, time_misc_a, mk_w1, mk_w2, time_misc_k, w_receptance, w_key, w_value, w_output, ln_w, ln_b):
            B_, T_, C_ = x.shape
            xprev = jnp.concatenate([jnp.zeros_like(x[:, :1]), x[:, :-1]], axis=1)
            xx = xprev - x
            mix_in = jnp.tanh((x + xx * time_maa_x) @ time_maa_w1)
            mix = jnp.einsum('btfd,fdc->fbtc', mix_in.reshape(B_, T_, 4, D_MIX), time_maa_w2)
            mrg, mwa, mk_, mv_ = (mix[0], mix[1], mix[2], mix[3])
            xrg = x + xx * (time_maa_rg + mrg)
            xwa = x + xx * (time_maa_wa + mwa)
            xk = x + xx * (time_maa_k + mk_)
            xv = x + xx * (time_maa_v + mv_)
            r = xrg @ w_receptance.T
            w = -jax.nn.softplus(-(time_decay + jnp.tanh(xwa @ time_decay_w1) @ time_decay_w2)) - 0.5
            k = xk @ w_key.T
            v = xv @ w_value.T
            g = jnp.tanh(xrg @ gate_w1) @ gate_w2
            kk = k + jnp.tanh(xk @ time_kkk_w1) @ time_kkk_w2
            kk4 = kk.reshape(B_, T_, H, N)
            kk4 = kk4 / jnp.maximum(jnp.linalg.norm(kk4, axis=-1, keepdims=True), 1e-12)
            kk = kk4.reshape(B_, T_, C_)
            a = jax.nn.sigmoid(time_aaaaa + xwa @ time_aaa_w1 @ time_aaa_w2)
            ma = jax.nn.sigmoid(time_misc_a + xwa @ ma_w1 @ ma_w2)
            k = k * ma + k * a * (1.0 - ma)
            mk2 = jax.nn.sigmoid(time_misc_k + xk @ mk_w1 @ mk_w2)
            k = k * jnp.exp(jnp.minimum(w * mk2, 0.0))
            y = wkv7(r, w, k, v, -kk, kk * a)
            yh = y.reshape(B_ * T_, H, N)
            mu = yh.mean(-1, keepdims=True)
            var = yh.var(-1, keepdims=True)
            yh = (yh - mu) * lax.rsqrt(var + EPS)
            y = (yh.reshape(B_ * T_, C_) * ln_w + ln_b).reshape(B_, T_, C_)
            rr = r.reshape(B_, T_, H, N)
            kr = k.reshape(B_, T_, H, N)
            vr = v.reshape(B_, T_, H, N)
            y = y + ((rr * kr * time_faaaa).sum(-1, keepdims=True) * vr).reshape(B_, T_, C_)
            return y * g @ w_output.T
        return _forward(x, time_maa_x, time_maa_rg, time_maa_wa, time_maa_k, time_maa_v, time_maa_w1, time_maa_w2, time_decay, time_decay_w1, time_decay_w2, time_faaaa, time_aaaaa, time_aaa_w1, time_aaa_w2, time_kkk_w1, time_kkk_w2, gate_w1, gate_w2, ma_w1, ma_w2, time_misc_a, mk_w1, mk_w2, time_misc_k, w_receptance, w_key, w_value, w_output, ln_w, ln_b)

    def _L0_ffn_ref(x, w_gate, w_up, w_down):
        import jax, jax.numpy as jnp
        import numpy as np
        DIM = 256
        HIDDEN = 768
        SCALE = 1.0 / 127.0

        def _dequant(w_int, dtype):
            return w_int.astype(dtype) * jnp.asarray(SCALE, dtype)
        wg = _dequant(w_gate, x.dtype)
        wu = _dequant(w_up, x.dtype)
        wd = _dequant(w_down, x.dtype)
        gate = jnp.einsum('bsd,hd->bsh', x, wg)
        up = jnp.einsum('bsd,hd->bsh', x, wu)
        h = jax.nn.silu(gate) * up
        return jnp.einsum('bsh,dh->bsd', h, wd)
    x = L0_attn_x
    xn = _layernorm(x, axis=-1)
    s = _L0_attn_ref(xn, L0_attn_time_maa_x, L0_attn_time_maa_rg, L0_attn_time_maa_wa, L0_attn_time_maa_k, L0_attn_time_maa_v, L0_attn_time_maa_w1, L0_attn_time_maa_w2, L0_attn_time_decay, L0_attn_time_decay_w1, L0_attn_time_decay_w2, L0_attn_time_faaaa, L0_attn_time_aaaaa, L0_attn_time_aaa_w1, L0_attn_time_aaa_w2, L0_attn_time_kkk_w1, L0_attn_time_kkk_w2, L0_attn_gate_w1, L0_attn_gate_w2, L0_attn_ma_w1, L0_attn_ma_w2, L0_attn_time_misc_a, L0_attn_mk_w1, L0_attn_mk_w2, L0_attn_time_misc_k, L0_attn_w_receptance, L0_attn_w_key, L0_attn_w_value, L0_attn_w_output, L0_attn_ln_w, L0_attn_ln_b)
    g = _silu(_L0_ffn_ref(xn, L0_ffn_w_gate, L0_ffn_w_up, L0_ffn_w_down))
    x = x + s * g
    return x

_drawn_inputs = setup_inputs


def setup_inputs(seed=0):
    import zlib

    import numpy as np

    out = dict(_drawn_inputs(seed))
    spreads = {'L0_attn_time_aaaaa': (0.0, 0.8),
     'L0_attn_time_misc_a': (0.0, 0.746),
     'L0_attn_time_misc_k': (0.0, 0.1),
     'L0_attn_ln_w': (1.0, 0.2),
     'L0_attn_ln_b': (0.0, 0.1)}
    factors = {'L0_attn_time_maa_wa': 8.0,
     'L0_attn_time_decay_w1': 4.478,
     'L0_attn_time_decay_w2': 4.528,
     'L0_attn_time_faaaa': 31.778,
     'L0_attn_time_aaa_w1': 8.0,
     'L0_attn_time_aaa_w2': 8.0,
     'L0_attn_ma_w1': 8.0,
     'L0_attn_ma_w2': 8.0,
     'L0_attn_mk_w1': 5.97,
     'L0_attn_mk_w2': 5.925}
    for name, (base, spread) in spreads.items():
        noise = np.random.default_rng([zlib.crc32(name.encode()), seed]).standard_normal(out[name].shape)
        drawn = base * np.exp(spread * noise) if base else spread * noise
        out[name] = jnp.asarray(drawn.astype(out[name].dtype))
    for name, factor in factors.items():
        out[name] = (out[name] * factor).astype(out[name].dtype)
    return out
```

```python
from contextlib import ExitStack

import numpy as np

import concourse.bass as bass
from concourse import mybir

F32 = mybir.dt.float32
I32 = mybir.dt.int32
U32 = mybir.dt.uint32
ACT = mybir.ActivationFunctionType
ALU = mybir.AluOpType
AX = mybir.AxisListType

B, T, C = 2, 4096, 256
H, N = 4, 64
NH = C // 128
TT_ = 256
COLS = B * TT_
NT = T // TT_
L = 32
BL = 8
NJ = L // BL
NQ = COLS // L
NP = NQ // 2
HQ = NH * NQ
QC = NQ // B
NM = COLS // 128
DH = 768
NF = DH // 128
NLANE = 2 * NQ * H
MAXDECAY = 20.0
LN_EPS, GN_EPS = 1e-5, 0.00064

WCOL, _at = {}, 0
for _n, _w in (("w1", 2 * 128), ("w2", 256), ("wr", 512), ("wk", 512), ("wv", 512), ("wo", 512),
               ("wa1", 2 * 112), ("wk1", 2 * 48), ("wa2", 256), ("wk2", 256), ("g1", 2 * 128), ("g2", 256)):
    WCOL[_n] = (_at, _at + _w)
    _at += _w
WTOT = _at
VEC = ("maa_x", "maa_rg", "maa_wa", "maa_k", "maa_v", "decay", "aaaaa", "misc_a", "misc_k", "faaaa", "ln_w", "ln_b")
CCOL, _at = {}, 0
for _n, _w in (("ident", 128), ("bd", 128), ("scan", 512), ("am0", 256), ("ti", 512)):
    CCOL[_n] = (_at, _at + _w)
    _at += _w
CTOT = _at

PAR = 1
NB = 4
ENG = ("pe", "act", "dve", "pool")
DMAS = ("xld", "awr", "ard", "twr", "trd", "ost")


class Progress:

    def __init__(self, nc, sems):
        self.nc, self.sems = nc, sems
        self.eng = {"pe": nc.tensor, "act": nc.scalar, "dve": nc.vector, "pool": nc.gpsimd, "sp": nc.sync}

    def section(self):
        self.n, self.seen = {k: 0 for k in self.sems}, {}

    def done(self, who, instruction):
        step = 16 if who in DMAS else 1
        instruction.then_inc(self.sems[who], step)
        self.n[who] += step
        return (who, self.n[who])

    def wait(self, eng, *marks):
        for m in marks:
            if m is None:
                continue
            who, n = m
            if self.seen.get((eng, who), 0) >= n:
                continue
            self.seen[(eng, who)] = n
            self.eng[eng].wait_ge(self.sems[who], n)

    def end(self):
        for eng in self.eng:
            for who in self.sems:
                if self.n[who]:
                    self.wait(eng, (who, self.n[who]))
        self.nc.all_engine_barrier()
        for who in self.sems:
            self.nc.sync.sem_clear(self.sems[who])
        self.nc.all_engine_barrier()


def program(nc, d):
    with ExitStack() as ctx:
        def sb(name, shape, dt=F32):
            return ctx.enter_context(nc.sbuf_tensor(name, shape, dt))

        def ps(name):
            return ctx.enter_context(nc.psum_tensor(name, [128, 512], F32))

        W = sb("W", [128, WTOT])
        vec = sb("vec", [128, len(VEC), NH])
        nvec = sb("nvec", [128, len(VEC), NH])
        con = sb("con", [128, CTOT])
        mask = sb("mask", [128, 256], U32)
        eps = sb("eps", [128, 4])
        wg = sb("wg", [128, NH, DH])
        wu = sb("wu", [128, NH, DH])
        wd = sb("wd", [128, NF, C])

        def wt(name):
            a, b = WCOL[name]
            return W[:, a:b]

        def cst(name):
            a, b = CCOL[name]
            return con[:, a:b]

        w1, wr, wk, wv, wo, wa1, wk1, g1 = (
            wt(n).rearrange("p (h n) -> p h n", h=NH) for n in ("w1", "wr", "wk", "wv", "wo", "wa1", "wk1", "g1"))
        w2, wa2, wk2, g2 = wt("w2"), wt("wa2"), wt("wk2"), wt("g2")
        ident, bd, scanm, am0, ti = (cst(n) for n in ("ident", "bd", "scan", "am0", "ti"))

        def v(name, h):
            return vec[:, VEC.index(name), h:h + 1]

        def nv(name, h):
            return nvec[:, VEC.index(name), h:h + 1]

        xtok = [sb(f"xtok{i}", [128, NM, C]) for i in range(PAR)]
        hat = [sb(f"hat{i}", [128, HQ, 2, L]) for i in range(PAR)]
        KT = [sb(f"KT{i}", [128, NP, NH, 128]) for i in range(PAR)]
        VU = [sb(f"VU{i}", [128, NP, C]) for i in range(PAR)]
        AM = [sb(f"AM{i}", [128, NP, 256]) for i in range(PAR)]
        TT = [sb(f"TT{i}", [128, NP * H, L]) for i in range(PAR)]
        CT = [sb(f"CT{i}", [128, HQ]) for i in range(PAR)]
        bv = [sb(f"bv{i}", [128, NH, COLS]) for i in range(PAR)]
        gT = [sb(f"gT{i}", [128, NH, COLS]) for i in range(PAR)]
        fsil = [sb(f"fsil{i}", [128, NM, C]) for i in range(PAR)]

        carry = sb("carry", [128, NH, B, 1])
        xT = sb("xT", [128, NH, B, TT_ + 1])
        bns = sb("bns", [128, NM, 6])
        mv = sb("mv", [128, NM, 2])
        rstd = sb("rstd", [128, NM])
        big = [sb(f"big{i}", [128, NH, COLS]) for i in range(10)]
        vd = sb("vd", [128, NH, NQ, 2, L])
        small = sb("small", [128, COLS])
        sml2 = sb("sml2", [128, COLS])
        KS = [sb(f"KS{i}", [128, QC, NJ * 2 * L]) for i in range(2)]
        KE = [sb(f"KE{i}", [128, QC, 2 * L]) for i in range(2)]
        qpad = [sb(f"qpad{i}", [128, QC, NJ, 2, 2, BL]) for i in range(2)]
        FL = sb("FL", [128, HQ, 25])
        EF = sb("EF", [128, HQ, 25])
        AL = big[0][:, :, :].rearrange("p h (a t) -> p (h a) t", t=L)
        TL = big[1][:, 0, :].rearrange("p (j t) -> p j t", t=L)
        prod = big[1][:, 1, :]
        hT = [big[2 + n // 2][:, n % 2, :] for n in range(NF)]
        sg = sb("sg", [128, COLS])
        ST = sb("ST", [128, B, NH, N])
        rhs = sb("rhs", [128, 512])
        Y = sb("Y", [128, NM * H, N])
        st1 = sb("st1", [128, NM * H])
        st2 = sb("st2", [128, NM * H])
        yg = sb("yg", [128, NH, COLS])
        yb = sb("yb", [128, NH, COLS])
        sq = yb[:, :, :].rearrange("p h (g n) -> p (h g) n", n=N)

        bank = [ps(f"bank{i}") for i in range(NB)]
        RY = ctx.enter_context(nc.psum_tensor("RY", [128, 2, 512], F32))
        PU, PS = ps("PU"), ps("PS")

        sems = {k: ctx.enter_context(nc.semaphore(f"s_{k}")) for k in ENG + DMAS}
        s_init = ctx.enter_context(nc.semaphore("s_init"))
        s_set = ctx.enter_context(nc.semaphore("s_set"))
        s_setp = ctx.enter_context(nc.semaphore("s_setp"))
        P = Progress(nc, sems)
        pe, act, dve, pool, sp = nc.tensor, nc.scalar, nc.vector, nc.gpsimd, nc.sync
        wait, done = P.wait, P.done

        sp.dma_start(con[:, :], d["con"]).then_inc(s_init, 16)
        sp.dma_start(vec[:, :, :], d["vec"]).then_inc(s_init, 16)
        sp.dma_start(mask[:, :], d["mask"]).then_inc(s_init, 16)
        sp.dma_start(W[:, :], d["W"]).then_inc(s_init, 16)
        ints = [big[i][:, :, :].rearrange("p h n -> p (h n)").bitcast(I32) for i in range(5)]
        nin = 64
        for i, (name, rows) in enumerate((("w_gate", NH * DH), ("w_up", NH * DH), ("w_down", NF * C))):
            for a in range(0, rows, 768):
                t = ints[(2 * i + a // 768) % 5]
                if 2 * i + a // 768 < 5:
                    act.dma_start(t[:, 0:768], d[name][:, a:a + 768]).then_inc(s_init, 16)
                    nin += 16
        for e in (pe, act, dve, pool):
            e.wait_ge(s_init, nin)
        fdst = [w[:, :, :].rearrange("p a b -> p (a b)") for w in (wg, wu, wd)]
        for k in range(5):
            dve.tensor_scalar(fdst[k // 2][:, 768 * (k % 2):768 * (k % 2) + 768], ints[k][:, 0:768],
                              1.0 / 127.0, None, ALU.mult).then_inc(s_set, 1)
        act.wait_ge(s_set, 5)
        act.dma_start(ints[0][:, 0:768], d["w_down"][:, 768:1536]).then_inc(s_init, 16)
        dve.wait_ge(s_init, nin + 16)
        dve.tensor_scalar(fdst[2][:, 768:1536], ints[0][:, 0:768], 1.0 / 127.0, None, ALU.mult).then_inc(s_set, 1)
        dve.tensor_scalar(nvec[:, :, :], vec[:, :, :], -1.0, None, ALU.mult).then_inc(s_set, 1)
        setup = 7
        for value, col in ((LN_EPS, 0), (GN_EPS, 1), (1.0, 2), (0.0, 3)):
            dve.memset(eps[:, col:col + 1], value).then_inc(s_set, 1)
            setup += 1
        for t in (ST[:, :, :, :], carry[:, :, :, :], FL[:, :, :], KS[0][:, :, :], KS[1][:, :, :],
                  qpad[0][:, :, :, :, :, :], qpad[1][:, :, :, :, :, :]):
            dve.memset(t, 0.0).then_inc(s_set, 1)
            setup += 1
        for i in range(PAR):
            for p in range(NP):
                pool.tensor_copy(AM[i][:, p, :], am0).then_inc(s_setp, 1)
        for e in (pe, act, dve, pool, sp):
            e.wait_ge(s_set, setup)
            e.wait_ge(s_setp, PAR * NP)

        ring = {"next": 0, "free": [None] * NB}

        def take():
            i = ring["next"]
            ring["next"] = (i + 1) % NB
            wait("pe", ring["free"][i])
            return i

        def project(i, weights, x, rows=128, base=0):
            for h in range(NH):
                m = pe.matmul(bank[i][base:base + rows, :], weights[:, h, :], x[:, h, :], start=(h == 0), stop=(h == NH - 1))
            return m

        x_in, x_out = d["x"], d["out"]

        def front(t, par):
            X = xtok[par]
            (xx, xm, xrg, xwa, xk, xv, rT, kT, tmp, na) = big
            ld = None
            for b in range(B):
                ld = done("xld", sp.dma_start(X[:, 2 * b:2 * b + 2, :],
                                              x_in[b, bass.ds(t * TT_, TT_), :].rearrange("(m p) c -> p m c", p=128)))
            wait("dve", ld)
            for m in range(NM):
                s = done("dve", dve.bn_stats(bns[:, m, :], X[:, m, :]))
            wait("dve", s)
            for m in range(NM):
                s = done("dve", dve.bn_aggr(mv[:, m, :], bns[:, m, :]))
            wait("act", s)
            a = done("act", act.activation(rstd[:, :], mv[:, :, 1], ACT.Ln, bias=eps[:, 0:1]))
            wait("act", a)
            a = done("act", act.activation(rstd[:, :], rstd[:, :], ACT.Exp, scale=-0.5))
            wait("dve", a)
            xn = xm[:, :, :].rearrange("p h n -> p (h n)").rearrange("p (m c) -> p m c", m=NM)
            for m in range(NM):
                s = done("dve", dve.tensor_scalar(xn[:, m, :], X[:, m, :], mv[:, m, 0:1], rstd[:, m:m + 1],
                                                  ALU.subtract, ALU.mult))
            yield
            wait("pe", s)
            c0 = done("pool", pool.tensor_copy(xT[:, :, :, 0:1], carry[:, :, :, :]))
            for h in range(NH):
                i = take()
                for m in range(NM):
                    q = pe.transpose(bank[i][:, 128 * m:128 * m + 128], xn[:, m, 128 * h:128 * h + 128], ident)
                q = done("pe", q)
                wait("act", q)
                a = done("act", act.activation(xT[:, h, :, 1:TT_ + 1], bank[i][:, :].rearrange("p (b n) -> p b n", b=B), ACT.Copy))
                ring["free"][i] = a
            xt_ready = a
            x_now = xT[:, :, :, 1:TT_ + 1]
            wait("pool", c0, a)
            done("pool", pool.tensor_copy(carry[:, :, :, :], xT[:, :, :, TT_:TT_ + 1]))
            split = "p (b n) -> p b n"
            wait("dve", c0, a)
            for h in range(NH):
                s = done("dve", dve.tensor_tensor(xx[:, h, :].rearrange(split, b=B), xT[:, h, :, 0:TT_], x_now[:, h], ALU.subtract))
            wait("dve", s)
            for h in range(NH):
                s = done("dve", dve.scalar_tensor_tensor(out=xm[:, h, :].rearrange(split, b=B), in0=xx[:, h, :].rearrange(split, b=B),
                                                         scalar=v("maa_x", h), in1=x_now[:, h], op0=ALU.mult, op1=ALU.add))
            yield
            i = take()
            wait("pe", s)
            q = done("pe", project(i, w1, xm))
            wait("act", q)
            a = done("act", act.activation(small[:, :], bank[i][:, :], ACT.Tanh))
            ring["free"][i] = a
            wait("pe", a)
            ready = {}
            tmps = (tmp, na)
            use = [None, None]
            for n, (f, dst, maa) in enumerate(((1, xwa, "maa_wa"), (2, xk, "maa_k"), (0, xrg, "maa_rg"), (3, xv, "maa_v"))):
                w = tmps[n % 2]
                for h in range(NH):
                    i = take()
                    q = done("pe", pe.matmul(bank[i][:, :], w2[32 * f:32 * f + 32, 128 * h:128 * h + 128],
                                             small[32 * f:32 * f + 32, :], start=True, stop=True))
                    wait("dve", q, use[n % 2])
                    s = done("dve", dve.scalar_tensor_tensor(out=w[:, h, :], in0=bank[i][:, :], scalar=v(maa, h),
                                                             in1=xx[:, h, :], op0=ALU.add, op1=ALU.mult))
                    ring["free"][i] = s
                    wait("pool", s)
                    g = done("pool", pool.tensor_tensor(dst[:, h, :].rearrange(split, b=B), w[:, h, :].rearrange(split, b=B),
                                                        x_now[:, h], ALU.add))
                use[n % 2] = g
                ready[f] = g
                yield
            i = take()
            wait("pe", ready[1])
            q = done("pe", project(i, wa1, xwa, rows=112))
            wait("act", q)
            a1 = done("act", act.activation(sml2[0:64, :], bank[i][0:64, :], ACT.Tanh))
            a = done("act", act.activation(sml2[64:112, :], bank[i][64:112, :], ACT.Copy))
            ring["free"][i] = a
            wait("pe", a)
            az, rz = xm, xx
            for h in range(NH):
                i = take()
                q = done("pe", pe.matmul(bank[i][:, :], wa2[0:64, 128 * h:128 * h + 128], sml2[0:64, :], start=True, stop=True))
                wait("act", q, ready[3])
                done("act", act.activation(az[:, h, :], bank[i][:, :], ACT.Abs, bias=v("decay", h)))
                a = done("act", act.activation(rz[:, h, :], bank[i][:, :], ACT.Relu, bias=nv("decay", h), scale=-1.0))
                ring["free"][i] = a
                i = take()
                q = done("pe", pe.matmul(bank[i][:, :], wa2[64:80, 128 * h:128 * h + 128], sml2[64:80, :], start=True, stop=True))
                wait("act", q, ready[3])
                a = done("act", act.activation(na[:, h, :], bank[i][:, :], ACT.Sigmoid, bias=nv("aaaaa", h), scale=-1.0))
                ring["free"][i] = a
            yield
            nma = xwa
            for h in range(NH):
                i = take()
                q = done("pe", pe.matmul(bank[i][:, :], wa2[96:112, 128 * h:128 * h + 128], sml2[96:112, :], start=True, stop=True))
                wait("act", q)
                a = done("act", act.activation(nma[:, h, :], bank[i][:, :], ACT.Sigmoid, bias=nv("misc_a", h), scale=-1.0))
                ring["free"][i] = a
            wait("pool", a)
            mix_a = nma
            nn = done("pool", pool.tensor_tensor(mix_a[:, :, :], na[:, :, :], nma[:, :, :], ALU.mult))
            yield
            wait("pe", ready[2])
            kq = []
            for h in range(NH):
                i = take()
                q = done("pe", project(i, wk[:, :, 128 * h:128 * h + 128], xk))
                wait("act", q)
                a = done("act", act.activation(kT[:, h, :], bank[i][:, :], ACT.Copy))
                ring["free"][i] = a
            k_ready = a
            i = take()
            q = done("pe", project(i, wk1, xk, rows=48))
            xk_free = q
            wait("act", q, )
            done("act", act.activation(small[0:16, :], bank[i][0:16, :], ACT.Tanh))
            a = done("act", act.activation(small[32:48, :], bank[i][32:48, :], ACT.Copy))
            ring["free"][i] = a
            wait("pe", a)
            kk, mk = tmp, xk
            for h in range(NH):
                i = take()
                q = done("pe", pe.matmul(bank[i][:, :], wk2[0:16, 128 * h:128 * h + 128], small[0:16, :], start=True, stop=True))
                wait("dve", q, k_ready)
                s = done("dve", dve.tensor_tensor(kk[:, h, :], bank[i][:, :], kT[:, h, :], ALU.add))
                ring["free"][i] = s
                i = take()
                q = done("pe", pe.matmul(bank[i][:, :], wk2[32:48, 128 * h:128 * h + 128], small[32:48, :], start=True, stop=True))
                wait("act", q)
                a = done("act", act.activation(mk[:, h, :], bank[i][:, :], ACT.Sigmoid, bias=v("misc_k", h)))
                ring["free"][i] = a
            kk_ready, mk_ready = s, a
            yield
            wait("pe", ready[0])
            for h in range(NH):
                i = take()
                q = done("pe", project(i, wr[:, :, 128 * h:128 * h + 128], xrg))
                wait("act", q)
                a = done("act", act.activation(rT[:, h, :], bank[i][:, :], ACT.Copy))
                ring["free"][i] = a
            r_ready = a
            i = take()
            q = done("pe", project(i, g1, xrg))
            xrg_free = q
            wait("act", q)
            a = done("act", act.activation(sml2[:, :], bank[i][:, :], ACT.Tanh))
            ring["free"][i] = a
            wait("pe", a)
            for h in range(NH):
                i = take()
                q = done("pe", pe.matmul(bank[i][:, :], g2[:, 128 * h:128 * h + 128], sml2[:, :], start=True, stop=True))
                wait("act", q)
                a = done("act", act.activation(gT[par][:, h, :], bank[i][:, :], ACT.Copy))
                ring["free"][i] = a
            yield
            wait("pe", ready[3])
            for h in range(NH):
                i = take()
                q = done("pe", project(i, wv[:, :, 128 * h:128 * h + 128], xv))
                wait("act", q)
                a = done("act", act.activation(vd[:, h], bank[i][:, :].rearrange("p (q t) -> p q t", t=L).unsqueeze(2)
                                               .to_broadcast([128, NQ, 2, L]), ACT.Copy))
                ring["free"][i] = a
            v_ready = a
            xv_free = q
            wait("pe", a)
            for p2 in range(NP // 2):
                i = take()
                for n in range(2):
                    for h in range(NH):
                        q0 = 2 * (2 * p2 + n)
                        q = pe.transpose(bank[i][:, 256 * n + 128 * h:256 * n + 128 * h + 128],
                                         vd[:, h, q0:q0 + 2].rearrange("p q d t -> p (q d t)"), ident)
                q = done("pe", q)
                wait("act", q)
                a = done("act", act.activation(VU[par][:, 2 * p2:2 * p2 + 2, :], bank[i][:, :].rearrange("p (n c) -> p n c", n=2), ACT.Copy))
                ring["free"][i] = a
            yield
            wait("act", a)
            a = done("act", act.activation(az[:, :, :], az[:, :, :], ACT.Exp, scale=-1.0))
            wait("act", a)
            a = done("act", act.activation(az[:, :, :], az[:, :, :], ACT.Ln, bias=eps[:, 2:3]))
            wait("dve", a)
            s = done("dve", dve.scalar_tensor_tensor(out=rz[:, :, :], in0=az[:, :, :], scalar=0.5, in1=rz[:, :, :], op0=ALU.add, op1=ALU.add))
            wait("dve", s)
            nd = az
            s = done("dve", dve.tensor_scalar(nd[:, :, :], rz[:, :, :], MAXDECAY, None, ALU.min))
            cs = xrg
            wait("dve", s, xrg_free)
            for h in range(NH):
                s = done("dve", dve.tensor_tensor_scan(cs[:, h, :], scanm, nd[:, h, :], 0.0, ALU.mult, ALU.add))
            cs_ready = s
            wait("pool", s, mk_ready)
            g = done("pool", pool.tensor_tensor(mk[:, :, :], mk[:, :, :], rz[:, :, :], ALU.mult))
            wait("act", g)
            em_ready = done("act", act.activation(mk[:, :, :], mk[:, :, :], ACT.Exp, scale=-1.0))
            wait("act", kk_ready, xv_free)
            sqk = xv
            a = done("act", act.activation(sqk[:, :, :], kk[:, :, :], ACT.Square))
            wait("pe", a)
            rn = rz
            for h in range(NH):
                i = take()
                q = done("pe", pe.matmul(bank[i][:, :], bd, sqk[:, h, :], start=True, stop=True))
                wait("dve", q, g)
                s = done("dve", dve.tensor_scalar(rn[:, h, :], bank[i][:, :], 1e-24, None, ALU.max))
                ring["free"][i] = s
            wait("act", s)
            a = done("act", act.activation(rn[:, :, :], rn[:, :, :], ACT.Ln))
            wait("act", a)
            a = done("act", act.activation(rn[:, :, :], rn[:, :, :], ACT.Exp, scale=-0.5))
            yield
            wait("dve", nn, k_ready)
            s = done("dve", dve.scalar_tensor_tensor(out=mix_a[:, :, :], in0=mix_a[:, :, :], scalar=1.0, in1=kT[:, :, :], op0=ALU.subtract, op1=ALU.mult))
            wait("dve", s, em_ready)
            k_fin = done("dve", dve.scalar_tensor_tensor(out=kT[:, :, :], in0=mix_a[:, :, :], scalar=-1.0, in1=mk[:, :, :], op0=ALU.mult, op1=ALU.mult))
            wait("pool", a)
            kk_fin = done("pool", pool.tensor_tensor(kk[:, :, :], kk[:, :, :], rn[:, :, :], ALU.mult))
            wait("dve", kk_fin)
            bneg = na
            b_fin = done("dve", dve.scalar_tensor_tensor(out=bneg[:, :, :], in0=na[:, :, :], scalar=1.0, in1=kk[:, :, :], op0=ALU.subtract, op1=ALU.mult))
            rk = xv
            wait("dve", k_fin, r_ready, q)
            for h in range(NH):
                s = done("dve", dve.scalar_tensor_tensor(out=rk[:, h, :], in0=rT[:, h, :], scalar=v("faaaa", h), in1=kT[:, h, :], op0=ALU.mult, op1=ALU.mult))
            wait("pe", s)
            for h in range(NH):
                i = take()
                q = done("pe", pe.matmul(bank[i][:, :], bd, rk[:, h, :], start=True, stop=True))
                wait("dve", q, v_ready)
                s = done("dve", dve.tensor_tensor(bv[par][:, h, :].rearrange("p (q t) -> p q t", t=L),
                                                     bank[i][:, :].rearrange("p (q t) -> p q t", t=L), vd[:, h, :, 0, :], ALU.mult))
                ring["free"][i] = s
            rk_free = q
            yield
            grp = "p h (g e) -> p (h g) e"
            csb = cs[:, :, :].rearrange(grp, e=BL)
            ndb = nd[:, :, :].rearrange(grp, e=BL)
            G = HQ * NJ
            dm, e2, e3 = mk, mix_a, rn
            dmb, e3b = (z[:, :, :].rearrange(grp, e=BL) for z in (dm, e3))
            wait("dve", k_fin, cs_ready)
            s1 = done("dve", dve.tensor_tensor(dmb, csb, csb[:, :, 3:4].to_broadcast([128, G, BL]), ALU.subtract))
            wait("dve", s1, k_fin)
            wait("pool", kk_fin, s1)
            g3 = done("pool", pool.tensor_tensor(e3b, csb[:, :, BL - 1:BL].to_broadcast([128, G, BL]), csb, ALU.subtract))
            s2 = done("dve", dve.tensor_tensor(e2[:, :, :], dm[:, :, :], nd[:, :, :], ALU.subtract))
            c4 = cs[:, :, :].rearrange("p h (q j e) -> p (h q) j e", j=NJ, e=BL)
            s = done("dve", dve.tensor_copy(FL[:, :, 0:24].rearrange("p q (a b) -> p q a b", b=6)[:, :, :, 0:1], c4[:, :, :, 3:4]))
            FLv = FL[:, :, :].rearrange("p q (i j) -> p q i j", i=5)
            EFv = EF[:, :, :].rearrange("p q (i j) -> p q i j", i=5)
            for j in range(NJ - 1, -1, -1):
                wait("dve", s)
                s = done("dve", dve.tensor_tensor(FLv[:, :, j + 1:5, j:j + 1], FLv[:, :, j + 1:5, j + 1:j + 2],
                                                  c4[:, :, j, BL - 1:BL].unsqueeze(2).to_broadcast([128, HQ, 4 - j, 1]), ALU.add))
            wait("act", s)
            ef = done("act", act.activation(EF[:, :, :], FL[:, :, :], ACT.Exp, scale=-1.0))
            wait("act", s2)
            xa = done("act", act.activation(e2[:, :, :], e2[:, :, :], ACT.Exp, scale=-1.0))
            ekey = nd
            wait("act", s2)
            xk_ = done("act", act.activation(ekey[:, :, :], dm[:, :, :], ACT.Exp))
            wait("act", xk_)
            xr = done("act", act.activation(dm[:, :, :], dm[:, :, :], ACT.Exp, scale=-1.0))
            wait("act", g3)
            xs = done("act", act.activation(e3[:, :, :], e3[:, :, :], ACT.Exp, scale=-1.0))
            yield
            wait("dve", xa)
            qa = done("dve", dve.tensor_tensor(e2[:, :, :], e2[:, :, :], kk[:, :, :], ALU.mult))
            wait("pool", xr)
            qr = done("pool", pool.tensor_tensor(dm[:, :, :], dm[:, :, :], rT[:, :, :], ALU.mult))
            five = "p h (q j e) -> p (h q) j e"
            a5, r5, kin, bin_, ek5, sf5 = (z[:, :, :].rearrange(five, j=NJ, e=BL) for z in (e2, dm, kT, bneg, ekey, e3))
            wait("dve", qr, qa, ef)
            hv = hat[par][:, :, :, :].rearrange("p q x (j e) -> p q x j e", e=BL)
            first = EFv[:, :, 0:NJ, 0:1].to_broadcast([128, HQ, NJ, BL])
            for x, own_q in ((0, a5), (1, r5)):
                s = done("dve", dve.tensor_tensor(hv[:, :, x], own_q, first, ALU.mult))
            done("dve", dve.tensor_copy(CT[par][:, :], EFv[:, :, NJ, 0]))
            wait("pool", qa, qr, ef, xk_, xs, b_fin)
            wait("act", qa, qr)
            wait("dve", xk_, xs, k_fin, b_fin)
            yield
            read = [None, None]
            for qt in range(NH * B):
                h, b, u = qt // B, qt % B, qt % 2
                qs = slice(QC * qt, QC * qt + QC)
                K, Q = KS[u], qpad[u]
                wait("dve", read[u])
                wait("pool", read[u])
                wait("act", read[u])
                for hh in range(2):
                    p0 = 64 * hh
                    g = done("pool", pool.tensor_copy(Q[p0:p0 + 64, :, :, hh, 0, :], a5[p0:p0 + 64, qs]))
                    wait("pool", g)
                    a = done("act", act.activation(Q[p0:p0 + 64, :, :, hh, 1, :], r5[p0:p0 + 64, qs], ACT.Copy))
                for x, z, who, eng in ((0, kin, "dve", dve), (1, bin_, "pool", pool)):
                    whole = K[:, :, :]
                    own = bass.AP(tensor=whole.tensor, offset=whole.offset + L * x,
                                  ap=[list(whole.ap[0]), [NJ * 2 * L, QC], [2 * L + BL, NJ], [1, BL]])
                    done(who, eng.tensor_tensor(own, z[:, qs], ek5[:, qs], ALU.mult))
                    wait(who, done(who, eng.tensor_tensor(z[:, qs], z[:, qs], sf5[:, qs], ALU.mult)))
                for i4 in range(1, NJ + 1):
                    fac = EFv[:, qs, i4, 1:i4 + 1].unsqueeze(3).to_broadcast([128, QC, i4, BL])
                    for x, z, who, eng in ((0, kin, "dve", dve), (1, bin_, "pool", pool)):
                        buf, at = (K, 2 * L * i4 + L * x) if i4 < NJ else (KE[u], L * x)
                        o = buf[:, :, at:at + BL * i4].rearrange("p q (j e) -> p q j e", e=BL)
                        m = done(who, eng.tensor_tensor(o, z[:, qs, 0:i4, :], fac, ALU.mult))
                        if x:
                            g = m
                        else:
                            s = m
                wait("pe", a, g, s)
                i = take()
                for n in range(QC // 2):
                    for cp in range(2):
                        o = bank[i][64 * cp:64 * cp + 64, 128 * n:128 * n + 128].rearrange("p (x e) -> p x e", e=L)
                        for j in range(NJ):
                            q = pe.matmul(o[:, :, BL * j:BL * j + BL], K[:, 2 * n + cp, 64 * j:64 * j + 64],
                                          Q[:, 2 * n + cp, j, :, :, :].rearrange("p a b e -> p (a b) e"), start=True, stop=True)
                q = done("pe", q)
                wait("dve", q)
                pairs = slice(4 * b, 4 * b + 4)
                am_ready = done("dve", dve.copy_predicated(AM[par][:, pairs, 128 * h:128 * h + 128],
                                                           mask[:, 0:128].unsqueeze(1).to_broadcast([128, 4, 128]),
                                                           bank[i][:, :].rearrange("p (n c) -> p n c", n=4)))
                ring["free"][i] = am_ready
                i = take()
                for n in range(QC // 2):
                    q = pe.transpose(bank[i][:, 128 * n:128 * n + 128], KE[u][:, 2 * n:2 * n + 2, :].rearrange("p q n -> p (q n)"), ident)
                read[u] = q = done("pe", q)
                wait("act", q)
                a = done("act", act.activation(KT[par][:, pairs, h, :], bank[i][:, :].rearrange("p (n c) -> p n c", n=4), ACT.Copy))
                ring["free"][i] = a
                yield
            wait("sp", am_ready)
            for cp in range(2):
                for p in range(0, NP, 4):
                    src = AM[par][64 * cp + 32:64 * cp + 64, p:p + 4, :].rearrange("s p (h x t) -> s (p h) x t", h=H, x=2)
                    w = done("awr", sp.dma_start(d["scrA"][cp, :, p:p + 4].rearrange("s p h t -> s (p h) t"), src[:, :, 0, :]))
            wait("sp", w)
            for jh in range(2):
                for cp in range(2):
                    l0 = 64 * jh + 32 * cp
                    w = done("ard", sp.dma_start(AL[l0:l0 + 32, :, :], d["scrA"][cp].rearrange("s p h t -> (p h) s t")))
            yield
            s = done("dve", dve.tensor_copy(TL[:, :, :], ti.rearrange("p (j t) -> p j t", t=L)))
            wait("dve", w)
            for tt in range(1, L):
                pv = prod[:, 0:16 * (tt + 1)].rearrange("p (j s) -> p j s", s=tt + 1)
                wait("dve", s)
                s = done("dve", dve.tensor_tensor(pv, TL[:, :, 0:tt + 1],
                                                  AL[:, 0:tt + 1, tt].unsqueeze(1).to_broadcast([128, 16, tt + 1]), ALU.mult))
                wait("dve", s)
                s = done("dve", dve.tensor_reduce(TL[:, :, tt:tt + 1], pv, AX.X, ALU.add))
                if tt % 4 == 3:
                    yield
            wait("sp", s)
            w = done("twr", sp.dma_start(d["scrT"], TL[:, :, :]))
            wait("sp", w)
            for cp in range(2):
                for jh in range(2):
                    p0, l0 = 64 * cp + 16 * jh, 64 * jh + 32 * cp
                    w = done("trd", sp.dma_start(TT[par][p0:p0 + 16, :, :], d["scrT"][l0:l0 + 32].rearrange("l j t -> j l t")))
            yield

        def ffn(par):
            split = "p (b n) -> p b n"
            x_now = xT[:, :, :, 1:TT_ + 1]
            for n in range(NF):
                cols = slice(128 * n, 128 * n + 128)
                ig, iu = take(), take()
                q = None
                for i, w in ((ig, wg), (iu, wu)):
                    for h in range(NH):
                        q = pe.matmul(bank[i][:, :].rearrange(split, b=B), w[:, h, cols], x_now[:, h], start=(h == 0), stop=(h == NH - 1))
                    q = done("pe", q)
                wait("act", q)
                if n:
                    wait("act", s)
                a = done("act", act.activation(sg[:, :], bank[ig][:, :], ACT.Sigmoid))
                wait("dve", a)
                s = done("dve", dve.tensor_tensor(sg[:, :], sg[:, :], bank[ig][:, :], ALU.mult))
                ring["free"][ig] = s
                wait("dve", s, q)
                s = done("dve", dve.tensor_tensor(hT[n], sg[:, :], bank[iu][:, :], ALU.mult))
                ring["free"][iu] = s
                yield
            wait("pe", s)
            for m2 in range(NM // 2):
                i = take()
                for n2 in range(2):
                    m = 2 * m2 + n2
                    for n in range(NF):
                        q = pe.matmul(bank[i][:, 256 * n2:256 * n2 + 256], hT[n][:, 128 * m:128 * m + 128], wd[:, n, :],
                                      start=(n == 0), stop=(n == NF - 1))
                q = done("pe", q)
                wait("act", q, s)
                a = done("act", act.activation(sg[:, :], bank[i][:, :], ACT.Sigmoid))
                wait("dve", a)
                s = done("dve", dve.tensor_tensor(fsil[par][:, 2 * m2:2 * m2 + 2, :], sg[:, :].rearrange("p (m c) -> p m c", m=2),
                                                  bank[i][:, :].rearrange("p (m c) -> p m c", m=2), ALU.mult))
                ring["free"][i] = s
                yield

        def back(t, par):
            A, V = AM[par], VU[par]
            y_read = [None, None]
            upd = None
            rhs_free = None
            u_read = None
            for c in range(NQ // B):
                cp = c % 2
                p0 = 64 * cp
                wait("pe", y_read[cp], upd)
                for h in range(H):
                    h2, hh = h // 2, h % 2
                    for b in range(B):
                        q = pe.matmul(RY[p0:p0 + 64, hh, 128 * b + 64 * h2:128 * b + 64 * h2 + 64],
                                      hat[par][64 * hh:64 * hh + 64, h2 * NQ + b * QC + c, :, :].rearrange("p x t -> p (x t)"),
                                      ST[64 * hh:64 * hh + 64, b, h2, :], start=(b == 0 and h2 == 0), stop=False, skip_group_check=True)
                wait("pe", done("pe", q))
                for b in range(B):
                    pr = b * (NP // B) + c // 2
                    for h in range(H):
                        q = pe.matmul(RY[p0:p0 + 32, h % 2, 128 * b + 64 * (h // 2):128 * b + 64 * (h // 2) + 64],
                                      A[p0:p0 + 32, pr, 64 * h:64 * h + 32], V[p0:p0 + 32, pr, 64 * h:64 * h + 64],
                                      start=False, stop=True, skip_group_check=True)
                q = done("pe", q)
                wait("act", q, rhs_free)
                a = done("act", act.activation(rhs[p0:p0 + 32, :].rearrange("p (x n) -> p x n", x=2), RY[p0:p0 + 32, :, 0:256], ACT.Copy))
                yield
                wait("pe", a, u_read)
                for b in range(B):
                    pr = b * (NP // B) + c // 2
                    for h in range(H):
                        q = pe.matmul(PU[p0 + 32:p0 + 64, 256 * b + 64 * h:256 * b + 64 * h + 64], TT[par][p0:p0 + 32, pr * H + h, :],
                                      rhs[p0:p0 + 32, 256 * (h % 2) + 128 * b + 64 * (h // 2):256 * (h % 2) + 128 * b + 64 * (h // 2) + 64],
                                      start=True, stop=True)
                q = done("pe", q)
                rhs_free = q
                wait("dve", q)
                vu = V[:, :, :].rearrange("p (b n) c -> p b n c", b=B)
                u_read = done("dve", dve.tensor_copy(vu[p0 + 32:p0 + 64, :, c // 2, :], PU[p0 + 32:p0 + 64, :].rearrange("p (b c) -> p b c", b=B)))
                yield
                wait("pe", u_read)
                for b in range(B):
                    pr = b * (NP // B) + c // 2
                    for h in range(H):
                        h2, hh = h // 2, 64 * (h % 2)
                        q = pe.matmul(PS[hh:hh + 64, 128 * b + 64 * h2:128 * b + 64 * h2 + 64], KT[par][p0:p0 + 64, pr, h2, hh:hh + 64],
                                      V[p0:p0 + 64, pr, 64 * h:64 * h + 64], start=True, stop=True)
                q = done("pe", q)
                wait("dve", q)
                for b in range(B):
                    for h2 in range(NH):
                        k = h2 * NQ + b * (NQ // B) + c
                        upd = done("dve", dve.scalar_tensor_tensor(
                            out=ST[:, b, h2, :], in0=ST[:, b, h2, :], scalar=CT[par][:, k:k + 1],
                            in1=PS[:, 128 * b + 64 * h2:128 * b + 64 * h2 + 64], op0=ALU.mult, op1=ALU.add))
                for b in range(B):
                    pr = b * (NP // B) + c // 2
                    for h in range(H):
                        q = pe.matmul(RY[p0 + 32:p0 + 64, h % 2, 128 * b + 64 * (h // 2):128 * b + 64 * (h // 2) + 64], A[p0:p0 + 64, pr, 64 * h + 32:64 * h + 64], V[p0:p0 + 64, pr, 64 * h:64 * h + 64],
                                      start=False, stop=True, skip_group_check=True)
                q = done("pe", q)
                wait("act", q)
                r0 = 32 * (c % 4)
                yv = Y[:, :, :].rearrange("p (b m g x) n -> p b m g x n", b=B, m=NM // B, x=2)
                for x in range(2):
                    y_read[cp] = done("act", act.activation(yv[r0:r0 + 32, :, c // 4, :, x, :], RY[p0 + 32:p0 + 64, x, 0:256]
                                                            .rearrange("p (b g n) -> p b g n", b=B, g=NH), ACT.Copy))
                yield
            wait("dve", y_read[0], y_read[1])
            G = NM * H
            s = done("dve", dve.tensor_reduce(st1[:, :].unsqueeze(2), Y[:, :, :], AX.X, ALU.add))
            wait("dve", s)
            s = done("dve", dve.scalar_tensor_tensor(out=Y[:, :, :], in0=st1[:, :].unsqueeze(2).to_broadcast([128, G, N]), scalar=-1.0 / N,
                                                     in1=Y[:, :, :], op0=ALU.mult, op1=ALU.add))
            wait("act", s)
            a = done("act", act.activation(sq[:, :, :], Y[:, :, :], ACT.Square))
            wait("dve", a)
            s = done("dve", dve.tensor_reduce(st2[:, :].unsqueeze(2), sq[:, :, :], AX.X, ALU.add))
            wait("act", s)
            a = done("act", act.activation(st2[:, :], st2[:, :], ACT.Ln, bias=eps[:, 1:2], scale=1.0 / N))
            wait("act", a)
            a = done("act", act.activation(st2[:, :], st2[:, :], ACT.Exp, scale=-0.5))
            wait("pool", a)
            g = done("pool", pool.tensor_tensor(Y[:, :, :], Y[:, :, :], st2[:, :].unsqueeze(2).to_broadcast([128, G, N]), ALU.mult))
            yield
            wait("pe", g)
            ym = Y[:, :, :].rearrange("p (m h) n -> p m (h n)", h=H)
            for h in range(NH):
                i = take()
                for m in range(NM):
                    q = pe.transpose(bank[i][:, 128 * m:128 * m + 128], ym[:, m, 128 * h:128 * h + 128], ident)
                q = done("pe", q)
                wait("act", q)
                a = done("act", act.activation(yb[:, h, :], bank[i][:, :], ACT.Identity, bias=v("ln_b", h), scale=v("ln_w", h)))
                ring["free"][i] = a
                wait("pool", a)
                g = done("pool", pool.tensor_tensor(yb[:, h, :], yb[:, h, :], bv[par][:, h, :], ALU.add))
                wait("pool", g)
                g = done("pool", pool.tensor_tensor(yg[:, h, :], yb[:, h, :], gT[par][:, h, :], ALU.mult))
            yield
            wait("pe", g)
            for m2 in range(NM // 2):
                i = take()
                for n2 in range(2):
                    m = 2 * m2 + n2
                    for h in range(NH):
                        q = pe.matmul(bank[i][:, 256 * n2:256 * n2 + 256], yg[:, h, 128 * m:128 * m + 128], wo[:, h, :],
                                      start=(h == 0), stop=(h == NH - 1))
                q = done("pe", q)
                wait("dve", q)
                fs, xo = fsil[par][:, 2 * m2:2 * m2 + 2, :], xtok[par][:, 2 * m2:2 * m2 + 2, :]
                s = done("dve", dve.tensor_tensor(fs, fs, bank[i][:, :].rearrange("p (m c) -> p m c", m=2), ALU.mult))
                ring["free"][i] = s
                wait("pool", s)
                g = done("pool", pool.tensor_tensor(fs, fs, xo, ALU.add))
                wait("act", g)
                done("ost", act.dma_start(x_out[m2, bass.ds(t * TT_, TT_), :].rearrange("(m p) c -> p m c", p=128), fs))
                yield

        def run(*streams):
            lists = [(list_len, s) for list_len, s in streams]
            at = [0] * len(lists)
            alive = [True] * len(lists)
            while any(alive):
                k = min((i for i in range(len(lists)) if alive[i]), key=lambda i: (at[i] + 1) / lists[i][0])
                at[k] += 1
                if next(lists[k][1], 0) == 0:
                    alive[k] = False

        def section(*streams):
            P.section()
            ring["free"] = [None] * NB
            run(*streams)
            P.end()

        def chain(*gens):
            for g in gens:
                for _ in g:
                    yield 1

        with nc.Fori(0, NT) as i:
            section((1, chain(front(i, 0), ffn(0))))
            section((1, chain(back(i, 0))))


def pack(inputs, np):
    g = {k.removeprefix("L0_attn_").removeprefix("L0_ffn_"): np.asarray(a) for k, a in inputs.items()}
    W = np.zeros((128, WTOT), np.float32)

    def put(name, a, at=0, rows=0):
        lo = WCOL[name][0] + at
        W[rows:rows + a.shape[0], lo:lo + a.shape[1]] = a

    def halves(name, a, width=None, at=0):
        w = width or a.shape[1]
        for h in range(2):
            put(name, a[128 * h:128 * h + 128], at=h * w + at)

    halves("w1", g["time_maa_w1"])
    put("w2", g["time_maa_w2"].reshape(128, 256))
    for n, s in (("wr", "w_receptance"), ("wk", "w_key"), ("wv", "w_value"), ("wo", "w_output")):
        halves(n, g[s].T)
    for s, at in (("time_decay_w1", 0), ("time_aaa_w1", 64), ("ma_w1", 96)):
        halves("wa1", g[s], 112, at)
    for s, at in (("time_kkk_w1", 0), ("mk_w1", 32)):
        halves("wk1", g[s], 48, at)
    put("wa2", g["time_decay_w2"])
    put("wa2", g["time_aaa_w2"], rows=64)
    put("wa2", g["ma_w2"], rows=96)
    put("wk2", g["time_kkk_w2"])
    put("wk2", g["mk_w2"], rows=32)
    halves("g1", g["gate_w1"])
    put("g2", g["gate_w2"])
    names = {"maa_x": "time_maa_x", "maa_rg": "time_maa_rg", "maa_wa": "time_maa_wa", "maa_k": "time_maa_k", "maa_v": "time_maa_v",
             "decay": "time_decay", "aaaaa": "time_aaaaa", "misc_a": "time_misc_a", "misc_k": "time_misc_k", "faaaa": "time_faaaa"}
    vec = np.stack([g[names.get(n, n)].reshape(2, 128).T for n in VEC], axis=1)
    con = np.zeros((128, CTOT), np.float32)

    def const(name):
        a, b = CCOL[name]
        return con[:, a:b]

    mask = np.zeros((128, 256), np.uint32)
    p = np.arange(128)
    const("ident")[p, p] = 1
    const("bd")[:, :] = p[:, None] // 64 == p[None, :] // 64
    const("scan")[:, :] = np.arange(512)[None, :] % BL != 0
    key, s = p % 64 // 32, p % 32
    col = np.arange(256)
    xq, tq = col % 64 // 32, col % 32
    mask[:, :] = np.where(xq[None, :] == 0, s[:, None] < tq[None, :], s[:, None] <= tq[None, :])
    const("am0")[:, :] = (key[:, None] == 1) & (xq[None, :] == 0) & (s[:, None] == tq[None, :])
    j, t = np.arange(512) // 32, np.arange(512) % 32
    const("ti")[:, :] = (p[:, None] // 64) * 16 + j[None, :] == t[None, :]

    def fold(a):
        return np.ascontiguousarray(a.reshape(a.shape[0] // 128, 128, a.shape[1]).transpose(1, 0, 2).reshape(128, -1))

    return {"x": np.ascontiguousarray(g["x"]), "W": W, "vec": np.ascontiguousarray(vec), "con": con, "mask": mask,
            "w_gate": fold(g["w_gate"].T), "w_up": fold(g["w_up"].T), "w_down": fold(g["w_down"].T)}


def build(bacc, arrays):
    nc = bacc.Bacc("TRN2", target_bir_lowering=False, num_devices=1)
    d = {k: nc.dram_tensor(f"in_{k}", list(a.shape), mybir.dt.from_np(a.dtype), kind="ExternalInput").ap() for k, a in arrays.items()}
    d["out"] = nc.dram_tensor("out_0", [B, T, C], F32, kind="ExternalOutput").ap()
    d["scrA"] = nc.dram_tensor("scrA", [2, L, NP, H, L], F32, kind="Internal").ap()
    d["scrT"] = nc.dram_tensor("scrT", [NLANE, 16, L], F32, kind="Internal").ap()
    program(nc, d)
    return nc


def kernel(**inputs):
    import numpy as _np
    import concourse.bacc as _bacc
    from concourse.bass_utils import run_bass_kernel_spmd as _run

    arrays = pack(inputs, _np)
    nc = build(_bacc, arrays)
    r = _run(nc, [{f"in_{k}": a for k, a in arrays.items()}], core_ids=[0])
    return r.results[0]["out_0"]
```

```python
from contextlib import ExitStack

import numpy as np

import concourse.bass as bass
from concourse import mybir

F32 = mybir.dt.float32
I32 = mybir.dt.int32
BF16 = mybir.dt.bfloat16
U32 = mybir.dt.uint32
ACT = mybir.ActivationFunctionType
ALU = mybir.AluOpType
AX = mybir.AxisListType

B, T, C = 2, 4096, 256
H, N = 4, 64
NH = C // 128
TT_ = 256
COLS = B * TT_
NT = T // TT_
L = 32
BL = 8
NJ = L // BL
NQ = COLS // L
NP = NQ // 2
HQ = NH * NQ
QC = NQ // B
NM = COLS // 128
DH = 768
NF = DH // 128
NLANE = 2 * NQ * H
MAXDECAY = 20.0
LN_EPS, GN_EPS = 1e-5, 0.00064

WCOL, _at = {}, 0
for _n, _w in (("w1", 2 * 128), ("w2", 256), ("wr", 512), ("wk", 512), ("wv", 512), ("wo", 512),
               ("wa1", 2 * 112), ("wk1", 2 * 48), ("wa2", 256), ("wk2", 256), ("g1", 2 * 128), ("g2", 256)):
    WCOL[_n] = (_at, _at + _w)
    _at += _w
WTOT = _at
VEC = ("maa_x", "maa_rg", "maa_wa", "maa_k", "maa_v", "decay", "aaaaa", "misc_a", "misc_k", "faaaa", "ln_w", "ln_b")
CCOL, _at = {}, 0
for _n, _w in (("ident", 128), ("bd", 128), ("am0", 256), ("scan", 512), ("ti", 512)):
    CCOL[_n] = (_at, _at + _w)
    _at += _w
CTOT = _at

ORDER = "FFFFBFFFBBBNFBFBNFBFBFFBBBFBFNDFFDBNBFBBBFDBBBBFBFFBBBDFBFBNBBBFBBDFDBNBFFBNBBBFBFFBFNBBFBFBFBNFFBBFFFB"
NB = 4
ENG = ("pe", "act", "dve", "pool")
DMAS = ("xld", "xre", "awr", "ard", "twr", "trd", "ost")


class Progress:

    def __init__(self, nc, sems):
        self.nc, self.sems = nc, sems
        self.eng = {"pe": nc.tensor, "act": nc.scalar, "dve": nc.vector, "pool": nc.gpsimd, "sp": nc.sync}

    def section(self):
        self.n, self.seen = {k: 0 for k in self.sems}, {}

    def done(self, who, instruction):
        step = 16 if who in DMAS else 1
        instruction.then_inc(self.sems[who], step)
        self.n[who] += step
        return (who, self.n[who])

    def wait(self, eng, *marks):
        for m in marks:
            if m is None:
                continue
            who, n = m
            if self.seen.get((eng, who), 0) >= n:
                continue
            self.seen[(eng, who)] = n
            self.eng[eng].wait_ge(self.sems[who], n)

    def end(self):
        for eng in self.eng:
            for who in self.sems:
                if self.n[who]:
                    self.wait(eng, (who, self.n[who]))
        self.nc.all_engine_barrier()
        for who in self.sems:
            self.nc.sync.sem_clear(self.sems[who])
        self.nc.all_engine_barrier()


def program(nc, d):
    with ExitStack() as ctx:
        def sb(name, shape, dt=F32):
            return ctx.enter_context(nc.sbuf_tensor(name, shape, dt))

        def ps(name):
            return ctx.enter_context(nc.psum_tensor(name, [128, 512], F32))

        W = sb("W", [128, WTOT])
        vec = sb("vec", [128, len(VEC), NH])
        nvec = sb("nvec", [128, len(VEC), NH])
        con = sb("con", [128, 256])
        cb = sb("cb", [128, 1024], BF16)
        mask = sb("mask", [128, 128], U32)
        eps = sb("eps", [128, 4])
        wg = sb("wg", [128, NH, DH])
        wu = sb("wu", [128, NH, DH])
        wd = sb("wd", [128, NF, C])

        def wt(name):
            a, b = WCOL[name]
            return W[:, a:b]

        w1, wr, wk, wv, wo, wa1, wk1, g1 = (
            wt(n).rearrange("p (h n) -> p h n", h=NH) for n in ("w1", "wr", "wk", "wv", "wo", "wa1", "wk1", "g1"))
        w2, wa2, wk2, g2 = wt("w2"), wt("wa2"), wt("wk2"), wt("g2")
        ident, bd, scanm, ti = con[:, 0:128], con[:, 128:256], cb[:, 0:512], cb[:, 512:1024]

        def v(name, h):
            return vec[:, VEC.index(name), h:h + 1]

        def nv(name, h):
            return nvec[:, VEC.index(name), h:h + 1]

        xT2 = [sb(f"xT{i}", [128, NH, B, TT_ + 1]) for i in range(2)]
        hat = [sb(f"hat{i}", [128, HQ, 2, L]) for i in range(2)]
        KT = [sb(f"KT{i}", [128, NP, NH, 128]) for i in range(2)]
        VU = [sb(f"VU{i}", [128, NP, C]) for i in range(2)]
        AM = [sb(f"AM{i}", [128, NP, 256]) for i in range(2)]
        CT = [sb(f"CT{i}", [128, HQ]) for i in range(2)]
        bv = [sb(f"bv{i}", [128, NH, COLS]) for i in range(2)]
        gT = [sb(f"gT{i}", [128, NH, COLS]) for i in range(2)]

        bns = sb("bns", [128, NM, 6])
        mv = sb("mv", [128, NM, 2])
        rstd = sb("rstd", [128, NM])
        big = [sb(f"big{i}", [128, NH, COLS]) for i in range(6)]
        KSb = [sb(f"KS{i}", [128, QC, NJ * 2 * L]) for i in range(2)]
        KE = [sb(f"KE{i}", [128, QC, 2 * L]) for i in range(2)]
        qpad = [sb(f"qpad{i}", [128, QC, NJ, 2, 2, BL]) for i in range(2)]
        duo = [k[:, :, :].rearrange("p q n -> p (q n)").rearrange("p (a h n) -> p a h n", a=2, h=NH) for k in KSb]
        smalls = sb("smalls", [128, 2 * COLS])
        small, sml2 = smalls[:, 0:COLS], smalls[:, COLS:2 * COLS]
        FL = smalls[:, 0:25 * HQ].rearrange("p (q n) -> p q n", n=25)
        EF = sb("EF", [128, HQ, 25])
        hT = sb("hT", [128, NF, TT_])
        sg = sb("sg", [128, COLS])
        fsil = sb("fsil", [128, NM, C])
        TT = sb("TT", [128, NP * H, L])
        ST = sb("ST", [128, B, NH, N])
        rhs = sb("rhs", [128, 512])
        Y = sb("Y", [128, NM * H, N])
        AL = fsil[:, :, :].rearrange("p m c -> p (m c)").rearrange("p (s t) -> p s t", t=L)
        TL = Y[:, 0:8, :].rearrange("p g n -> p (g n)").rearrange("p (j t) -> p j t", t=L)
        prod = Y[:, 8:16, :].rearrange("p g n -> p (g n)")
        st1 = sb("st1", [128, NM * H])
        st2 = sb("st2", [128, NM * H])
        bank = [ps(f"bank{i}") for i in range(NB)]
        RY = ctx.enter_context(nc.psum_tensor("RY", [128, 2, 512], F32))
        PU, PS = ps("PU"), ps("PS")

        sems = {k: ctx.enter_context(nc.semaphore(f"s_{k}")) for k in ENG + DMAS}
        s_init = ctx.enter_context(nc.semaphore("s_init"))
        s_set = ctx.enter_context(nc.semaphore("s_set"))
        s_setp = ctx.enter_context(nc.semaphore("s_setp"))
        P = Progress(nc, sems)
        pe, act, dve, pool, sp = nc.tensor, nc.scalar, nc.vector, nc.gpsimd, nc.sync
        wait, done = P.wait, P.done

        sp.dma_start(con[:, :], d["con"][:, 0:256]).then_inc(s_init, 16)
        am0 = duo[0][:, 0, 0, 0:256]
        stage = duo[1][:, 0].rearrange("p h n -> p (h n)")
        sp.dma_start(am0, d["con"][:, 256:512]).then_inc(s_init, 16)
        sp.dma_start(stage, d["con"][:, 512:1536]).then_inc(s_init, 16)
        sp.dma_start(vec[:, :, :], d["vec"]).then_inc(s_init, 16)
        sp.dma_start(mask[:, :], d["mask"]).then_inc(s_init, 16)
        sp.dma_start(W[:, :], d["W"]).then_inc(s_init, 16)
        ints = [big[i][:, :, :].rearrange("p h n -> p (h n)").bitcast(I32) for i in range(5)]
        nin = 96
        for i, (name, rows) in enumerate((("w_gate", NH * DH), ("w_up", NH * DH), ("w_down", NF * C))):
            for a in range(0, rows, 768):
                t = ints[(2 * i + a // 768) % 5]
                if 2 * i + a // 768 < 5:
                    act.dma_start(t[:, 0:768], d[name][:, a:a + 768]).then_inc(s_init, 16)
                    nin += 16
        for e in (pe, act, dve, pool):
            e.wait_ge(s_init, nin)
        fdst = [w[:, :, :].rearrange("p a b -> p (a b)") for w in (wg, wu, wd)]
        for k in range(5):
            dve.tensor_scalar(fdst[k // 2][:, 768 * (k % 2):768 * (k % 2) + 768], ints[k][:, 0:768],
                              1.0 / 127.0, None, ALU.mult).then_inc(s_set, 1)
        act.wait_ge(s_set, 5)
        act.dma_start(ints[0][:, 0:768], d["w_down"][:, 768:1536]).then_inc(s_init, 16)
        dve.wait_ge(s_init, nin + 16)
        dve.tensor_scalar(fdst[2][:, 768:1536], ints[0][:, 0:768], 1.0 / 127.0, None, ALU.mult).then_inc(s_set, 1)
        dve.tensor_scalar(nvec[:, :, :], vec[:, :, :], -1.0, None, ALU.mult).then_inc(s_set, 1)
        dve.tensor_copy(cb[:, :], stage).then_inc(s_set, 1)
        setup = 8
        for value, col in ((LN_EPS, 0), (GN_EPS, 1), (1.0, 2), (0.0, 3)):
            dve.memset(eps[:, col:col + 1], value).then_inc(s_set, 1)
            setup += 1
        for t in (ST[:, :, :, :], xT2[1][:, :, :, TT_:TT_ + 1],
                  qpad[0][:, :, :, :, :, :], qpad[1][:, :, :, :, :, :]):
            dve.memset(t, 0.0).then_inc(s_set, 1)
            setup += 1
        for i in range(2):
            for p in range(NP):
                pool.tensor_copy(AM[i][:, p, :], am0).then_inc(s_setp, 1)
        for e in (pe, act, dve, pool, sp):
            e.wait_ge(s_set, setup)
            e.wait_ge(s_setp, 2 * NP)

        ring = {"next": 0, "free": [None] * NB}

        def take():
            i = ring["next"]
            ring["next"] = (i + 1) % NB
            wait("pe", ring["free"][i])
            return i

        def project(i, weights, x, rows=128, base=0):
            for h in range(NH):
                m = pe.matmul(bank[i][base:base + rows, :], weights[:, h, :], x[:, h, :], start=(h == 0), stop=(h == NH - 1))
            return m

        x_in, x_out = d["x"], d["out"]

        marks = {}

        def front(t, par):
            (xx, xm, xwa, xk, kT, na) = big
            xv, xrg = duo[0][:, 0], duo[0][:, 1]
            tmp, vdf = duo[1][:, 0], duo[1][:, 1]
            xT, before = xT2[par], xT2[1 - par]
            X = kT[:, :, :].rearrange("p h n -> p (h n)").rearrange("p (m c) -> p m c", m=NM)
            ld = None
            for b in range(B):
                ld = done("xld", sp.dma_start(X[:, 2 * b:2 * b + 2, :],
                                              x_in[b, bass.ds(t * TT_, TT_), :].rearrange("(m p) c -> p m c", p=128)))
            yield
            wait("dve", ld)
            for m in range(NM):
                s = done("dve", dve.bn_stats(bns[:, m, :], X[:, m, :]))
            wait("dve", s)
            for m in range(NM):
                s = done("dve", dve.bn_aggr(mv[:, m, :], bns[:, m, :]))
            yield
            wait("act", s)
            a = done("act", act.activation(rstd[:, :], mv[:, :, 1], ACT.Ln, bias=eps[:, 0:1]))
            wait("act", a)
            a = done("act", act.activation(rstd[:, :], rstd[:, :], ACT.Exp, scale=-0.5))
            yield
            wait("dve", a)
            xn = xm[:, :, :].rearrange("p h n -> p (h n)").rearrange("p (m c) -> p m c", m=NM)
            for m in range(NM):
                s = done("dve", dve.tensor_scalar(xn[:, m, :], X[:, m, :], mv[:, m, 0:1], rstd[:, m:m + 1],
                                                  ALU.subtract, ALU.mult))
            yield
            wait("pe", s)
            c0 = done("pool", pool.tensor_copy(xT[:, :, :, 0:1], before[:, :, :, TT_:TT_ + 1]))
            for h in range(NH):
                i = take()
                for m in range(NM):
                    q = pe.transpose(bank[i][:, 128 * m:128 * m + 128], xn[:, m, 128 * h:128 * h + 128], ident)
                q = done("pe", q)
                wait("act", q)
                a = done("act", act.activation(xT[:, h, :, 1:TT_ + 1], bank[i][:, :].rearrange("p (b n) -> p b n", b=B), ACT.Copy))
                ring["free"][i] = a
            x_now = xT[:, :, :, 1:TT_ + 1]
            yield
            wait("pool", a)
            split = "p (b n) -> p b n"
            wait("dve", c0, a)
            for h in range(NH):
                s = done("dve", dve.tensor_tensor(xx[:, h, :].rearrange(split, b=B), xT[:, h, :, 0:TT_], x_now[:, h], ALU.subtract))
            wait("dve", s)
            for h in range(NH):
                s = done("dve", dve.scalar_tensor_tensor(out=xm[:, h, :].rearrange(split, b=B), in0=xx[:, h, :].rearrange(split, b=B),
                                                         scalar=v("maa_x", h), in1=x_now[:, h], op0=ALU.mult, op1=ALU.add))
            yield
            i = take()
            wait("pe", s)
            q = done("pe", project(i, w1, xm))
            wait("act", q)
            a = done("act", act.activation(small[:, :], bank[i][:, :], ACT.Tanh))
            ring["free"][i] = a
            yield
            wait("pe", a)
            ready = {}
            tmps = (tmp, na)
            use = [None, None]
            for n, (f, dst, maa) in enumerate(((1, xwa, "maa_wa"), (2, xk, "maa_k"), (0, xrg, "maa_rg"), (3, xv, "maa_v"))):
                w = tmps[n % 2]
                for h in range(NH):
                    i = take()
                    q = done("pe", pe.matmul(bank[i][:, :], w2[32 * f:32 * f + 32, 128 * h:128 * h + 128],
                                             small[32 * f:32 * f + 32, :], start=True, stop=True))
                    wait("dve", q, use[n % 2])
                    s = done("dve", dve.scalar_tensor_tensor(out=w[:, h, :], in0=bank[i][:, :], scalar=v(maa, h),
                                                             in1=xx[:, h, :], op0=ALU.add, op1=ALU.mult))
                    ring["free"][i] = s
                    wait("pool", s)
                    g = done("pool", pool.tensor_tensor(dst[:, h, :].rearrange(split, b=B), w[:, h, :].rearrange(split, b=B),
                                                        x_now[:, h], ALU.add))
                use[n % 2] = g
                ready[f] = g
                yield
            i = take()
            wait("pe", ready[1])
            q = done("pe", project(i, wa1, xwa, rows=112))
            wait("act", q)
            a1 = done("act", act.activation(sml2[0:64, :], bank[i][0:64, :], ACT.Tanh))
            a = done("act", act.activation(sml2[64:112, :], bank[i][64:112, :], ACT.Copy))
            ring["free"][i] = a
            yield
            wait("pe", a)
            az, rz = xm, xx
            for h in range(NH):
                i = take()
                q = done("pe", pe.matmul(bank[i][:, :], wa2[0:64, 128 * h:128 * h + 128], sml2[0:64, :], start=True, stop=True))
                wait("act", q, ready[3])
                done("act", act.activation(az[:, h, :], bank[i][:, :], ACT.Abs, bias=v("decay", h)))
                a = done("act", act.activation(rz[:, h, :], bank[i][:, :], ACT.Relu, bias=nv("decay", h), scale=-1.0))
                ring["free"][i] = a
                i = take()
                q = done("pe", pe.matmul(bank[i][:, :], wa2[64:80, 128 * h:128 * h + 128], sml2[64:80, :], start=True, stop=True))
                wait("act", q, ready[3])
                a = done("act", act.activation(na[:, h, :], bank[i][:, :], ACT.Sigmoid, bias=nv("aaaaa", h), scale=-1.0))
                ring["free"][i] = a
            marks["z"] = a
            yield
            nma = xwa
            for h in range(NH):
                i = take()
                q = done("pe", pe.matmul(bank[i][:, :], wa2[96:112, 128 * h:128 * h + 128], sml2[96:112, :], start=True, stop=True))
                wait("act", q)
                a = done("act", act.activation(nma[:, h, :], bank[i][:, :], ACT.Sigmoid, bias=nv("misc_a", h), scale=-1.0))
                ring["free"][i] = a
            wait("pool", a)
            mix_a = nma
            nn = done("pool", pool.tensor_tensor(mix_a[:, :, :], na[:, :, :], nma[:, :, :], ALU.mult))
            yield
            wait("pe", ready[2])
            kq = []
            for h in range(NH):
                i = take()
                q = done("pe", project(i, wk[:, :, 128 * h:128 * h + 128], xk))
                wait("act", q)
                a = done("act", act.activation(kT[:, h, :], bank[i][:, :], ACT.Copy))
                ring["free"][i] = a
            k_ready = a
            i = take()
            q = done("pe", project(i, wk1, xk, rows=48))
            xk_free = q
            wait("act", q, )
            done("act", act.activation(small[0:16, :], bank[i][0:16, :], ACT.Tanh))
            a = done("act", act.activation(small[32:48, :], bank[i][32:48, :], ACT.Copy))
            ring["free"][i] = a
            yield
            wait("pe", a)
            kk, mk = tmp, xk
            for h in range(NH):
                i = take()
                q = done("pe", pe.matmul(bank[i][:, :], wk2[0:16, 128 * h:128 * h + 128], small[0:16, :], start=True, stop=True))
                wait("dve", q, k_ready)
                s = done("dve", dve.tensor_tensor(kk[:, h, :], bank[i][:, :], kT[:, h, :], ALU.add))
                ring["free"][i] = s
                i = take()
                q = done("pe", pe.matmul(bank[i][:, :], wk2[32:48, 128 * h:128 * h + 128], small[32:48, :], start=True, stop=True))
                wait("act", q)
                a = done("act", act.activation(mk[:, h, :], bank[i][:, :], ACT.Sigmoid, bias=v("misc_k", h)))
                ring["free"][i] = a
            kk_ready, mk_ready = s, a
            yield
            wait("pe", ready[0])
            i = take()
            q = done("pe", project(i, g1, xrg))
            wait("act", q)
            a = done("act", act.activation(sml2[:, :], bank[i][:, :], ACT.Tanh))
            ring["free"][i] = a
            g_hidden = a
            yield
            wait("pe", ready[3])
            half = "p (q t) -> p q t"
            ii = []
            for h in range(NH):
                ii.append(take())
                q = done("pe", project(ii[h], wv[:, :, 128 * h:128 * h + 128], xv))
            marks["xv free"] = q
            for h in range(NH):
                vd = vdf.rearrange("p h n -> p (h n)").rearrange("p (q d t) -> p q d t", d=2, t=L)
                wait("act", q)
                done("act", act.activation(vd, bank[ii[h]][:, :].rearrange(half, t=L).unsqueeze(2).to_broadcast([128, NQ, 2, L]), ACT.Copy))
                a = done("act", act.activation(bv[par][:, h, :], bank[ii[h]][:, :], ACT.Copy))
                ring["free"][ii[h]] = a
                yield
                wait("pe", a)
                for p4 in range(0, NP, 4):
                    i = take()
                    for n in range(4):
                        q = pe.transpose(bank[i][:, 128 * n:128 * n + 128], vd[:, 2 * (p4 + n):2 * (p4 + n) + 2].rearrange("p q d t -> p (q d t)"), ident)
                    q = done("pe", q)
                    wait("act", q)
                    ring["free"][i] = done("act", act.activation(VU[par][:, p4:p4 + 4, 128 * h:128 * h + 128],
                                                                 bank[i][:, :].rearrange("p (n c) -> p n c", n=4), ACT.Copy))
            v_ready = a
            yield
            ii = []
            for h in range(NH):
                ii.append(take())
                q = done("pe", project(ii[h], wr[:, :, 128 * h:128 * h + 128], xrg))
            rT = xrg
            wait("act", q)
            for h in range(NH):
                a = done("act", act.activation(rT[:, h, :], bank[ii[h]][:, :], ACT.Copy))
                ring["free"][ii[h]] = a
            r_ready = a
            yield
            wait("pe", g_hidden)
            for h in range(NH):
                i = take()
                q = done("pe", pe.matmul(bank[i][:, :], g2[:, 128 * h:128 * h + 128], sml2[:, :], start=True, stop=True))
                wait("act", q)
                a = done("act", act.activation(gT[par][:, h, :], bank[i][:, :], ACT.Copy))
                ring["free"][i] = a
            marks["smalls free"] = q
            yield
            rz = xx
            wait("pool", marks["n"], mk_ready)
            g = done("pool", pool.tensor_tensor(mk[:, :, :], mk[:, :, :], rz[:, :, :], ALU.mult))
            wait("act", g)
            em_ready = done("act", act.activation(mk[:, :, :], mk[:, :, :], ACT.Exp, scale=-1.0))
            yield
            wait("act", kk_ready)
            sqk = vdf
            a = done("act", act.activation(sqk[:, :, :], kk[:, :, :], ACT.Square))
            yield
            wait("pe", a)
            rn = rz
            for h in range(NH):
                i = take()
                q = done("pe", pe.matmul(bank[i][:, :], bd, sqk[:, h, :], start=True, stop=True))
                wait("dve", q, g)
                s = done("dve", dve.tensor_scalar(rn[:, h, :], bank[i][:, :], 1e-24, None, ALU.max))
                ring["free"][i] = s
            wait("act", s)
            a = done("act", act.activation(rn[:, :, :], rn[:, :, :], ACT.Ln))
            wait("act", a)
            a = done("act", act.activation(rn[:, :, :], rn[:, :, :], ACT.Exp, scale=-0.5))
            yield
            wait("dve", nn, k_ready)
            s = done("dve", dve.scalar_tensor_tensor(out=mix_a[:, :, :], in0=mix_a[:, :, :], scalar=1.0, in1=kT[:, :, :], op0=ALU.subtract, op1=ALU.mult))
            wait("dve", s, em_ready)
            k_fin = done("dve", dve.scalar_tensor_tensor(out=kT[:, :, :], in0=mix_a[:, :, :], scalar=-1.0, in1=mk[:, :, :], op0=ALU.mult, op1=ALU.mult))
            wait("pool", a)
            kk_fin = done("pool", pool.tensor_tensor(kk[:, :, :], kk[:, :, :], rn[:, :, :], ALU.mult))
            wait("dve", kk_fin)
            bneg = na
            b_fin = done("dve", dve.scalar_tensor_tensor(out=bneg[:, :, :], in0=na[:, :, :], scalar=1.0, in1=kk[:, :, :], op0=ALU.subtract, op1=ALU.mult))
            rk = vdf
            wait("dve", k_fin, r_ready, q)
            for h in range(NH):
                s = done("dve", dve.scalar_tensor_tensor(out=rk[:, h, :], in0=rT[:, h, :], scalar=v("faaaa", h), in1=kT[:, h, :], op0=ALU.mult, op1=ALU.mult))
            yield
            wait("pe", s)
            for h in range(NH):
                i = take()
                q = done("pe", pe.matmul(bank[i][:, :], bd, rk[:, h, :], start=True, stop=True))
                wait("dve", q, v_ready)
                s = done("dve", dve.tensor_tensor(bv[par][:, h, :], bank[i][:, :], bv[par][:, h, :], ALU.mult))
                ring["free"][i] = s
            rk_free = q
            yield
            grp = "p h (g e) -> p (h g) e"
            cs, nd, cs_ready = xv, az, marks["cs"]
            csb = cs[:, :, :].rearrange(grp, e=BL)
            G = HQ * NJ
            dm, e2, e3 = mk, mix_a, rn
            dmb, e3b = (z[:, :, :].rearrange(grp, e=BL) for z in (dm, e3))
            wait("dve", k_fin, cs_ready)
            s1 = done("dve", dve.tensor_tensor(dmb, csb, csb[:, :, 3:4].to_broadcast([128, G, BL]), ALU.subtract))
            wait("dve", s1, k_fin)
            wait("pool", kk_fin, s1)
            g3 = done("pool", pool.tensor_tensor(e3b, csb[:, :, BL - 1:BL].to_broadcast([128, G, BL]), csb, ALU.subtract))
            s2 = done("dve", dve.tensor_tensor(e2[:, :, :], dm[:, :, :], nd[:, :, :], ALU.subtract))
            ef = marks["ef"]
            EFv = EF[:, :, :].rearrange("p q (i j) -> p q i j", i=5)
            wait("act", s2)
            xa = done("act", act.activation(e2[:, :, :], e2[:, :, :], ACT.Exp, scale=-1.0))
            ekey = nd
            wait("act", s2)
            xk_ = done("act", act.activation(ekey[:, :, :], dm[:, :, :], ACT.Exp))
            wait("act", xk_)
            xr = done("act", act.activation(dm[:, :, :], dm[:, :, :], ACT.Exp, scale=-1.0))
            wait("act", g3)
            xs = done("act", act.activation(e3[:, :, :], e3[:, :, :], ACT.Exp, scale=-1.0))
            yield
            wait("dve", xa)
            qa = done("dve", dve.tensor_tensor(e2[:, :, :], e2[:, :, :], kk[:, :, :], ALU.mult))
            wait("pool", xr)
            qr = done("pool", pool.tensor_tensor(dm[:, :, :], dm[:, :, :], rT[:, :, :], ALU.mult))
            five = "p h (q j e) -> p (h q) j e"
            a5, r5, kin, bin_, ek5, sf5 = (z[:, :, :].rearrange(five, j=NJ, e=BL) for z in (e2, dm, kT, bneg, ekey, e3))
            yield
            wait("dve", qr, qa, ef)
            hv = hat[par][:, :, :, :].rearrange("p q x (j e) -> p q x j e", e=BL)
            first = EFv[:, :, 0:NJ, 0:1].to_broadcast([128, HQ, NJ, BL])
            for x, own_q in ((0, a5), (1, r5)):
                s = done("dve", dve.tensor_tensor(hv[:, :, x], own_q, first, ALU.mult))
            done("dve", dve.tensor_copy(CT[par][:, :], EFv[:, :, NJ, 0]))
            wait("pool", qa, qr, ef, xk_, xs, b_fin, rk_free, s)
            wait("act", qa, qr)
            wait("dve", xk_, xs, k_fin, b_fin, rk_free)
            yield
            read = [None, None]
            made = {}

            def keys(qt):
                u = qt % 2
                qs = slice(QC * qt, QC * qt + QC)
                K, Q = KSb[u], qpad[u]
                wait("dve", read[u])
                wait("pool", read[u])
                wait("act", read[u])
                for hh in range(2):
                    p0 = 64 * hh
                    g = done("pool", pool.tensor_copy(Q[p0:p0 + 64, :, :, hh, 0, :], a5[p0:p0 + 64, qs]))
                    wait("pool", g)
                    a = done("act", act.activation(Q[p0:p0 + 64, :, :, hh, 1, :], r5[p0:p0 + 64, qs], ACT.Copy))
                for x, z, who, eng in ((0, kin, "dve", dve), (1, bin_, "pool", pool)):
                    whole = K[:, :, :]
                    own = bass.AP(tensor=whole.tensor, offset=whole.offset + L * x,
                                  ap=[list(whole.ap[0]), [NJ * 2 * L, QC], [2 * L + BL, NJ], [1, BL]])
                    done(who, eng.tensor_tensor(own, z[:, qs], ek5[:, qs], ALU.mult))
                    wait(who, done(who, eng.tensor_tensor(z[:, qs], z[:, qs], sf5[:, qs], ALU.mult)))
                for i4 in range(1, NJ + 1):
                    fac = EFv[:, qs, i4, 1:i4 + 1].unsqueeze(3).to_broadcast([128, QC, i4, BL])
                    for x, z, who, eng in ((0, kin, "dve", dve), (1, bin_, "pool", pool)):
                        buf, at = (K, 2 * L * i4 + L * x) if i4 < NJ else (KE[u], L * x)
                        o = buf[:, :, at:at + BL * i4].rearrange("p q (j e) -> p q j e", e=BL)
                        m = done(who, eng.tensor_tensor(o, z[:, qs, 0:i4, :], fac, ALU.mult))
                        made[qt, x] = m
                made[qt, 2], made[qt, 3] = a, g

            def matrices(qt):
                h, b, u = qt // B, qt % B, qt % 2
                K, Q = KSb[u], qpad[u]
                wait("pe", *(made[qt, n] for n in range(4)))
                i = take()
                for n in range(QC // 2):
                    for cp in range(2):
                        o = bank[i][64 * cp:64 * cp + 64, 128 * n:128 * n + 128].rearrange("p (x e) -> p x e", e=L)
                        for j in range(NJ):
                            q = pe.matmul(o[:, :, BL * j:BL * j + BL], K[:, 2 * n + cp, 64 * j:64 * j + 64],
                                          Q[:, 2 * n + cp, j, :, :, :].rearrange("p a b e -> p (a b) e"), start=True, stop=True)
                q = done("pe", q)
                wait("dve", q)
                pairs = slice(4 * b, 4 * b + 4)
                am_ready = done("dve", dve.copy_predicated(AM[par][:, pairs, 128 * h:128 * h + 128],
                                                           mask[:, 0:128].unsqueeze(1).to_broadcast([128, 4, 128]),
                                                           bank[i][:, :].rearrange("p (n c) -> p n c", n=4)))
                ring["free"][i] = am_ready
                i = take()
                for n in range(QC // 2):
                    q = pe.transpose(bank[i][:, 128 * n:128 * n + 128], KE[u][:, 2 * n:2 * n + 2, :].rearrange("p q n -> p (q n)"), ident)
                read[u] = q = done("pe", q)
                wait("act", q)
                a = done("act", act.activation(KT[par][:, pairs, h, :], bank[i][:, :].rearrange("p (n c) -> p n c", n=4), ACT.Copy))
                ring["free"][i] = a
                return am_ready

            keys(0)
            yield
            for qt in range(NH * B):
                if qt + 1 < NH * B:
                    keys(qt + 1)
                    yield
                am_ready = matrices(qt)
                yield

        def decays(par):
            az, rz = big[1], big[0]
            wait("act", marks["z"])
            a = done("act", act.activation(az[:, :, :], az[:, :, :], ACT.Exp, scale=-1.0))
            wait("act", a)
            a = done("act", act.activation(az[:, :, :], az[:, :, :], ACT.Ln, bias=eps[:, 2:3]))
            yield
            wait("dve", a)
            s = done("dve", dve.scalar_tensor_tensor(out=rz[:, :, :], in0=az[:, :, :], scalar=0.5, in1=rz[:, :, :], op0=ALU.add, op1=ALU.add))
            wait("dve", s)
            nd = az
            marks["n"] = s
            s = done("dve", dve.tensor_scalar(nd[:, :, :], rz[:, :, :], MAXDECAY, None, ALU.min))
            yield
            cs = duo[0][:, 0]
            wait("dve", s, marks["xv free"])
            for h in range(NH):
                s = done("dve", dve.tensor_tensor_scan(cs[:, h, :], scanm, nd[:, h, :], 0.0, ALU.mult, ALU.add))
            marks["cs"] = s
            yield
            wait("pool", marks["smalls free"])
            zeroed = done("pool", pool.memset(FL[:, :, :], 0.0))
            wait("dve", zeroed, s)
            c4 = cs[:, :, :].rearrange("p h (q j e) -> p (h q) j e", j=NJ, e=BL)
            s = done("dve", dve.tensor_copy(FL[:, :, 0:24].rearrange("p q (a b) -> p q a b", b=6)[:, :, :, 0:1], c4[:, :, :, 3:4]))
            FLv = FL[:, :, :].rearrange("p q (i j) -> p q i j", i=5)
            for j in range(NJ - 1, -1, -1):
                wait("dve", s)
                s = done("dve", dve.tensor_tensor(FLv[:, :, j + 1:5, j:j + 1], FLv[:, :, j + 1:5, j + 1:j + 2],
                                                  c4[:, :, j, BL - 1:BL].unsqueeze(2).to_broadcast([128, HQ, 4 - j, 1]), ALU.add))
                if j == 2:
                    yield
            yield
            wait("act", s)
            marks["ef"] = done("act", act.activation(EF[:, :, :], FL[:, :, :], ACT.Exp, scale=-1.0))

        def ffn(par):
            s = last = None
            for b in range(B):
                x_now = xT2[par][:, :, b, 1:TT_ + 1]
                for n in range(0, NF, 2):
                    ig, iu = take(), take()
                    for i, w in ((ig, wg), (iu, wu)):
                        for n2 in range(2):
                            for h in range(NH):
                                q = pe.matmul(bank[i][:, TT_ * n2:TT_ * n2 + TT_], w[:, h, 128 * (n + n2):128 * (n + n2) + 128],
                                              x_now[:, h], start=(h == 0), stop=(h == NH - 1))
                        q = done("pe", q)
                    wait("act", q, s)
                    a = done("act", act.activation(sg[:, :], bank[ig][:, :], ACT.Sigmoid))
                    wait("dve", a, last)
                    s = done("dve", dve.tensor_tensor(sg[:, :], sg[:, :], bank[ig][:, :], ALU.mult))
                    ring["free"][ig] = s
                    wait("dve", s, q)
                    s = done("dve", dve.tensor_tensor(hT[:, n:n + 2, :], sg[:, :].rearrange("p (n c) -> p n c", n=2),
                                                      bank[iu][:, :].rearrange("p (n c) -> p n c", n=2), ALU.mult))
                    ring["free"][iu] = s
                    yield
                wait("pe", s)
                i = take()
                for m in range(2):
                    for n in range(NF):
                        q = pe.matmul(bank[i][:, 256 * m:256 * m + 256], hT[:, n, 128 * m:128 * m + 128], wd[:, n, :],
                                      start=(n == 0), stop=(n == NF - 1))
                last = q = done("pe", q)
                wait("act", q, s)
                a = done("act", act.activation(sg[:, :], bank[i][:, :], ACT.Sigmoid))
                wait("dve", a, marks["inverted"])
                s = done("dve", dve.tensor_tensor(fsil[:, 2 * b:2 * b + 2, :], sg[:, :].rearrange("p (m c) -> p m c", m=2),
                                                  bank[i][:, :].rearrange("p (m c) -> p m c", m=2), ALU.mult))
                ring["free"][i] = s
                marks["ffn"] = s
                yield

        def back(t, par, other):
            for cp in range(2):
                for p in range(0, NP, 4):
                    src = AM[par][64 * cp + 32:64 * cp + 64, p:p + 4, :].rearrange("s p (h x t) -> s (p h) x t", h=H, x=2)
                    w = done("awr", sp.dma_start(d["scrA"][cp, :, p:p + 4].rearrange("s p h t -> s (p h) t"), src[:, :, 0, :]))
            wait("sp", w)
            for jh in range(2):
                for cp in range(2):
                    l0 = 64 * jh + 32 * cp
                    w = done("ard", sp.dma_start(AL[l0:l0 + 32, :, :], d["scrA"][cp].rearrange("s p h t -> (p h) s t")))
            yield
            s = done("dve", dve.tensor_copy(TL[:, :, :], ti.rearrange("p (j t) -> p j t", t=L)))
            wait("dve", w)
            for tt in range(1, L):
                pv = prod[:, 0:16 * (tt + 1)].rearrange("p (j s) -> p j s", s=tt + 1)
                wait("dve", s)
                s = done("dve", dve.tensor_tensor(pv, TL[:, :, 0:tt + 1],
                                                  AL[:, 0:tt + 1, tt].unsqueeze(1).to_broadcast([128, 16, tt + 1]), ALU.mult))
                wait("dve", s)
                s = done("dve", dve.tensor_reduce(TL[:, :, tt:tt + 1], pv, AX.X, ALU.add))
                if tt % 3 == 0:
                    yield
            marks["inverted"] = s
            wait("sp", s)
            w = done("twr", sp.dma_start(d["scrT"], TL[:, :, :]))
            wait("sp", w)
            for cp in range(2):
                for jh in range(2):
                    p0, l0 = 64 * cp + 16 * jh, 64 * jh + 32 * cp
                    w = done("trd", sp.dma_start(TT[p0:p0 + 16, :, :], d["scrT"][l0:l0 + 32].rearrange("l j t -> j l t")))
            yield
            wait("pe", w)
            A, V = AM[par], VU[par]
            y_read = [None, None]
            upd = None
            rhs_free = None
            u_read = None
            av = {}

            def values(c):
                p0 = 64 * (c % 2)
                wait("pe", y_read[c % 2])
                for b in range(B):
                    pr = b * (NP // B) + c // 2
                    for h in range(H):
                        q = pe.matmul(RY[p0:p0 + 64, h % 2, 128 * b + 64 * (h // 2):128 * b + 64 * (h // 2) + 64],
                                      A[p0:p0 + 32, pr, 64 * h:64 * h + 64], V[p0:p0 + 32, pr, 64 * h:64 * h + 64],
                                      start=(b == 0 and h < 2), stop=True, skip_group_check=True)
                av[c] = done("pe", q)

            values(0)
            for c in range(NQ // B):
                cp = c % 2
                p0 = 64 * cp
                if upd:
                    yield
                wait("pe", av[c], upd)
                for h in range(H):
                    h2, hh = h // 2, h % 2
                    for b in range(B):
                        q = pe.matmul(RY[p0:p0 + 64, hh, 128 * b + 64 * h2:128 * b + 64 * h2 + 64],
                                      hat[par][64 * hh:64 * hh + 64, h2 * NQ + b * QC + c, :, :].rearrange("p x t -> p (x t)"),
                                      ST[64 * hh:64 * hh + 64, b, h2, :], start=False, stop=False, skip_group_check=True)
                q = done("pe", q)
                wait("act", q, rhs_free)
                a = done("act", act.activation(rhs[p0:p0 + 32, :].rearrange("p (x n) -> p x n", x=2), RY[p0:p0 + 32, :, 0:256], ACT.Copy))
                yield
                wait("pe", a, u_read)
                for b in range(B):
                    pr = b * (NP // B) + c // 2
                    for h in range(H):
                        q = pe.matmul(PU[p0 + 32:p0 + 64, 256 * b + 64 * h:256 * b + 64 * h + 64], TT[p0:p0 + 32, pr * H + h, :],
                                      rhs[p0:p0 + 32, 256 * (h % 2) + 128 * b + 64 * (h // 2):256 * (h % 2) + 128 * b + 64 * (h // 2) + 64],
                                      start=True, stop=True)
                q = done("pe", q)
                rhs_free = q
                if c + 1 < QC:
                    values(c + 1)
                wait("dve", q)
                vu = V[:, :, :].rearrange("p (b n) c -> p b n c", b=B)
                u_read = done("dve", dve.tensor_copy(vu[p0 + 32:p0 + 64, :, c // 2, :], PU[p0 + 32:p0 + 64, :].rearrange("p (b c) -> p b c", b=B)))
                yield
                wait("pe", u_read)
                for b in range(B):
                    pr = b * (NP // B) + c // 2
                    for h in range(H):
                        h2, hh = h // 2, 64 * (h % 2)
                        q = pe.matmul(PS[hh:hh + 64, 128 * b + 64 * h2:128 * b + 64 * h2 + 64], KT[par][p0:p0 + 64, pr, h2, hh:hh + 64],
                                      V[p0:p0 + 64, pr, 64 * h:64 * h + 64], start=True, stop=True)
                q = done("pe", q)
                wait("dve", q)
                for b in range(B):
                    for h2 in range(NH):
                        k = h2 * NQ + b * (NQ // B) + c
                        upd = done("dve", dve.scalar_tensor_tensor(
                            out=ST[:, b, h2, :], in0=ST[:, b, h2, :], scalar=CT[par][:, k:k + 1],
                            in1=PS[:, 128 * b + 64 * h2:128 * b + 64 * h2 + 64], op0=ALU.mult, op1=ALU.add))
                for b in range(B):
                    pr = b * (NP // B) + c // 2
                    for h in range(H):
                        q = pe.matmul(RY[p0 + 32:p0 + 64, h % 2, 128 * b + 64 * (h // 2):128 * b + 64 * (h // 2) + 64], 
                                      A[p0 + 32:p0 + 64, pr, 64 * h + 32:64 * h + 64], V[p0 + 32:p0 + 64, pr, 64 * h:64 * h + 64],
                                      start=False, stop=True, skip_group_check=True)
                q = done("pe", q)
                wait("act", q)
                r0 = 32 * (c % 4)
                yv = Y[:, :, :].rearrange("p (b m g x) n -> p b m g x n", b=B, m=NM // B, x=2)
                for x in range(2):
                    y_read[cp] = done("act", act.activation(yv[r0:r0 + 32, :, c // 4, :, x, :], RY[p0 + 32:p0 + 64, x, 0:256]
                                                            .rearrange("p (b g n) -> p b g n", b=B, g=NH), ACT.Copy))
                yield
            spare = hat[par][:, :, :, :].rearrange("p q x t -> p (q x t)")
            yb = spare[:, 0:NH * COLS].rearrange("p (h n) -> p h n", h=NH)
            sq = spare[:, NH * COLS:].rearrange("p (g n) -> p g n", n=N)
            wait("dve", y_read[0], y_read[1])
            G = NM * H
            s = done("dve", dve.tensor_reduce(st1[:, :].unsqueeze(2), Y[:, :, :], AX.X, ALU.add))
            wait("dve", s)
            s = done("dve", dve.scalar_tensor_tensor(out=Y[:, :, :], in0=st1[:, :].unsqueeze(2).to_broadcast([128, G, N]), scalar=-1.0 / N,
                                                     in1=Y[:, :, :], op0=ALU.mult, op1=ALU.add))
            wait("act", s)
            a = done("act", act.activation(sq, Y[:, :, :], ACT.Square))
            wait("dve", a)
            s = done("dve", dve.tensor_reduce(st2[:, :].unsqueeze(2), sq, AX.X, ALU.add))
            wait("act", s)
            a = done("act", act.activation(st2[:, :], st2[:, :], ACT.Ln, bias=eps[:, 1:2], scale=1.0 / N))
            wait("act", a)
            a = done("act", act.activation(st2[:, :], st2[:, :], ACT.Exp, scale=-0.5))
            wait("pool", a)
            g = done("pool", pool.tensor_tensor(Y[:, :, :], Y[:, :, :], st2[:, :].unsqueeze(2).to_broadcast([128, G, N]), ALU.mult))
            yield
            wait("pe", g)
            ym = Y[:, :, :].rearrange("p (m h) n -> p m (h n)", h=H)
            for h in range(NH):
                i = take()
                for m in range(NM):
                    q = pe.transpose(bank[i][:, 128 * m:128 * m + 128], ym[:, m, 128 * h:128 * h + 128], ident)
                q = done("pe", q)
                wait("act", q)
                a = done("act", act.activation(yb[:, h, :], bank[i][:, :], ACT.Identity, bias=v("ln_b", h), scale=v("ln_w", h)))
                ring["free"][i] = a
                wait("pool", a)
                g = done("pool", pool.tensor_tensor(yb[:, h, :], yb[:, h, :], bv[par][:, h, :], ALU.add))
                wait("pool", g)
                g = done("pool", pool.tensor_tensor(yb[:, h, :], yb[:, h, :], gT[par][:, h, :], ALU.mult))
            wait("sp", q)
            for b in range(B):
                x2 = done("xre", sp.dma_start(ym[:, 2 * b:2 * b + 2, :], x_in[b, bass.ds(t * TT_, TT_), :].rearrange("(m p) c -> p m c", p=128)))
            yield
            for _ in other:
                yield
            wait("pe", g)
            for m2 in range(NM // 2):
                i = take()
                for n2 in range(2):
                    m = 2 * m2 + n2
                    for h in range(NH):
                        q = pe.matmul(bank[i][:, 256 * n2:256 * n2 + 256], yb[:, h, 128 * m:128 * m + 128], wo[:, h, :],
                                      start=(h == 0), stop=(h == NH - 1))
                q = done("pe", q)
                wait("dve", q, marks["ffn"])
                fs, xo = fsil[:, 2 * m2:2 * m2 + 2, :], ym[:, 2 * m2:2 * m2 + 2, :]
                s = done("dve", dve.tensor_tensor(fs, fs, bank[i][:, :].rearrange("p (m c) -> p m c", m=2), ALU.mult))
                ring["free"][i] = s
                wait("pool", s, x2)
                g = done("pool", pool.tensor_tensor(fs, fs, xo, ALU.add))
                wait("act", g)
                done("ost", act.dma_start(x_out[m2, bass.ds(t * TT_, TT_), :].rearrange("(m p) c -> p m c", p=128), fs))
                yield

        def step(stream):
            for _ in stream:
                return True
            return False

        def run(streams):
            for name in ORDER:
                if name in streams and not step(streams[name]):
                    del streams[name]
            assert not streams

        def section(front_of=None, back_of=None):
            P.section()
            ring["free"] = [None] * NB
            marks.clear()
            streams = {}
            if front_of:
                streams["F"], streams["D"] = front(*front_of), decays(front_of[1])
            if back_of:
                streams["N"] = ffn(back_of[1])
                streams["B"] = back(*back_of, streams["N"])
            run(streams)
            P.end()

        section(front_of=(0, 0))
        with nc.Fori(0, NT // 2 - 1) as i:
            section(front_of=(2 * i + 1, 1), back_of=(2 * i, 0))
            section(front_of=(2 * i + 2, 0), back_of=(2 * i + 1, 1))
        section(front_of=(NT - 1, 1), back_of=(NT - 2, 0))
        section(back_of=(NT - 1, 1))


def pack(inputs, np):
    g = {k.removeprefix("L0_attn_").removeprefix("L0_ffn_"): np.asarray(a) for k, a in inputs.items()}
    W = np.zeros((128, WTOT), np.float32)

    def put(name, a, at=0, rows=0):
        lo = WCOL[name][0] + at
        W[rows:rows + a.shape[0], lo:lo + a.shape[1]] = a

    def halves(name, a, width=None, at=0):
        w = width or a.shape[1]
        for h in range(2):
            put(name, a[128 * h:128 * h + 128], at=h * w + at)

    halves("w1", g["time_maa_w1"])
    put("w2", g["time_maa_w2"].reshape(128, 256))
    for n, s in (("wr", "w_receptance"), ("wk", "w_key"), ("wv", "w_value"), ("wo", "w_output")):
        halves(n, g[s].T)
    for s, at in (("time_decay_w1", 0), ("time_aaa_w1", 64), ("ma_w1", 96)):
        halves("wa1", g[s], 112, at)
    for s, at in (("time_kkk_w1", 0), ("mk_w1", 32)):
        halves("wk1", g[s], 48, at)
    put("wa2", g["time_decay_w2"])
    put("wa2", g["time_aaa_w2"], rows=64)
    put("wa2", g["ma_w2"], rows=96)
    put("wk2", g["time_kkk_w2"])
    put("wk2", g["mk_w2"], rows=32)
    halves("g1", g["gate_w1"])
    put("g2", g["gate_w2"])
    names = {"maa_x": "time_maa_x", "maa_rg": "time_maa_rg", "maa_wa": "time_maa_wa", "maa_k": "time_maa_k", "maa_v": "time_maa_v",
             "decay": "time_decay", "aaaaa": "time_aaaaa", "misc_a": "time_misc_a", "misc_k": "time_misc_k", "faaaa": "time_faaaa"}
    vec = np.stack([g[names.get(n, n)].reshape(2, 128).T for n in VEC], axis=1)
    con = np.zeros((128, CTOT), np.float32)

    def const(name):
        a, b = CCOL[name]
        return con[:, a:b]

    mask = np.zeros((128, 128), np.uint32)
    p = np.arange(128)
    const("ident")[p, p] = 1
    const("bd")[:, :] = p[:, None] // 64 == p[None, :] // 64
    const("scan")[:, :] = np.arange(512)[None, :] % BL != 0
    key, s = p % 64 // 32, p % 32
    col = np.arange(256)
    xq, tq = col % 64 // 32, col % 32
    mask[:, :] = np.where(xq[None, :] == 0, s[:, None] < tq[None, :], s[:, None] <= tq[None, :])[:, 0:128]
    const("am0")[:, :] = (key[:, None] == 1) & (xq[None, :] == 0) & (s[:, None] == tq[None, :])
    j, t = np.arange(512) // 32, np.arange(512) % 32
    const("ti")[:, :] = (p[:, None] // 64) * 16 + j[None, :] == t[None, :]

    def fold(a):
        return np.ascontiguousarray(a.reshape(a.shape[0] // 128, 128, a.shape[1]).transpose(1, 0, 2).reshape(128, -1))

    return {"x": np.ascontiguousarray(g["x"]), "W": W, "vec": np.ascontiguousarray(vec), "con": con, "mask": mask,
            "w_gate": fold(g["w_gate"].T), "w_up": fold(g["w_up"].T), "w_down": fold(g["w_down"].T)}


def build(bacc, arrays):
    nc = bacc.Bacc("TRN2", target_bir_lowering=False, num_devices=1)
    d = {k: nc.dram_tensor(f"in_{k}", list(a.shape), mybir.dt.from_np(a.dtype), kind="ExternalInput").ap() for k, a in arrays.items()}
    d["out"] = nc.dram_tensor("out_0", [B, T, C], F32, kind="ExternalOutput").ap()
    d["scrA"] = nc.dram_tensor("scrA", [2, L, NP, H, L], F32, kind="Internal").ap()
    d["scrT"] = nc.dram_tensor("scrT", [NLANE, 16, L], F32, kind="Internal").ap()
    program(nc, d)
    return nc


def kernel(**inputs):
    import numpy as _np
    import concourse.bacc as _bacc
    from concourse.bass_utils import run_bass_kernel_spmd as _run

    arrays = pack(inputs, _np)
    nc = build(_bacc, arrays)
    r = _run(nc, [{f"in_{k}": a for k, a in arrays.items()}], core_ids=[0])
    return r.results[0]["out_0"]
```

```python
from contextlib import ExitStack

import numpy as np

import concourse.bass as bass
from concourse import mybir

F32 = mybir.dt.float32
I32 = mybir.dt.int32
BF16 = mybir.dt.bfloat16
U32 = mybir.dt.uint32
ACT = mybir.ActivationFunctionType
ALU = mybir.AluOpType
AX = mybir.AxisListType

B, T, C = 2, 4096, 256
H, N = 4, 64
NH = C // 128
TT_ = 256
COLS = B * TT_
NT = T // TT_
L = 32
BL = 8
NJ = L // BL
NQ = COLS // L
NP = NQ // 2
HQ = NH * NQ
QC = NQ // B
NM = COLS // 128
DH = 768
NF = DH // 128
NLANE = 2 * NQ * H
MAXDECAY = 20.0
LN_EPS, GN_EPS = 1e-5, 0.00064

WCOL, _at = {}, 0
for _n, _w in (("w1", 2 * 128), ("w2", 256), ("wr", 512), ("wk", 512), ("wv", 512), ("wo", 512),
               ("wa1", 2 * 112), ("wk1", 2 * 48), ("wa2", 256), ("wk2", 256), ("g1", 2 * 128), ("g2", 256)):
    WCOL[_n] = (_at, _at + _w)
    _at += _w
WTOT = _at
VEC = ("maa_x", "maa_rg", "maa_wa", "maa_k", "maa_v", "decay", "aaaaa", "misc_a", "misc_k", "faaaa", "ln_w", "ln_b")
CCOL, _at = {}, 0
for _n, _w in (("ident", 128), ("bd", 128), ("am0", 256), ("scan", 512), ("ti", 512)):
    CCOL[_n] = (_at, _at + _w)
    _at += _w
CTOT = _at

ORDER = ("BFNFFBFNBFBFFNFBFBFFBBFNFBNNFFFFFBBBNNFFFFNFNDFBNBNFBBBNDFBBFBBF"
         "BBBBFBBBBBFBFFDBDBBBBFBBDBNBBDBFBBBFBFBNBBBFLBBBFBBBFBBBLFNFFBFF"
         "LNBBLFFLFFLFDB")
NB = 4
ENG = ("pe", "act", "dve", "pool")
DMAS = ("xld", "xre", "awr", "ard", "twr", "trd", "ost")


class Progress:

    def __init__(self, nc, sems):
        self.nc, self.sems = nc, sems
        self.eng = {"pe": nc.tensor, "act": nc.scalar, "dve": nc.vector, "pool": nc.gpsimd, "sp": nc.sync}

    def section(self):
        self.n, self.seen = {k: 0 for k in self.sems}, {}

    def done(self, who, instruction):
        step = 16 if who in DMAS else 1
        instruction.then_inc(self.sems[who], step)
        self.n[who] += step
        return (who, self.n[who])

    def wait(self, eng, *marks):
        for m in marks:
            if m is None:
                continue
            who, n = m
            if self.seen.get((eng, who), 0) >= n:
                continue
            self.seen[(eng, who)] = n
            self.eng[eng].wait_ge(self.sems[who], n)

    def end(self):
        for eng in self.eng:
            for who in self.sems:
                if self.n[who]:
                    self.wait(eng, (who, self.n[who]))
        self.nc.all_engine_barrier()
        for who in self.sems:
            self.nc.sync.sem_clear(self.sems[who])
        self.nc.all_engine_barrier()


def program(nc, d):
    with ExitStack() as ctx:
        def sb(name, shape, dt=F32):
            return ctx.enter_context(nc.sbuf_tensor(name, shape, dt))

        def ps(name):
            return ctx.enter_context(nc.psum_tensor(name, [128, 512], F32))

        W = sb("W", [128, WTOT])
        vec = sb("vec", [128, len(VEC), NH])
        nvec = sb("nvec", [128, len(VEC), NH])
        con = sb("con", [128, 256])
        cb = sb("cb", [128, 1024], BF16)
        mask = sb("mask", [128, 128], U32)
        eps = sb("eps", [128, 4])
        wg = sb("wg", [128, NH, DH])
        wu = sb("wu", [128, NH, DH])
        wd = sb("wd", [128, NF, C])

        def wt(name):
            a, b = WCOL[name]
            return W[:, a:b]

        w1, wr, wk, wv, wo, wa1, wk1, g1 = (
            wt(n).rearrange("p (h n) -> p h n", h=NH) for n in ("w1", "wr", "wk", "wv", "wo", "wa1", "wk1", "g1"))
        w2, wa2, wk2, g2 = wt("w2"), wt("wa2"), wt("wk2"), wt("g2")
        ident, bd, scanm, ti = con[:, 0:128], con[:, 128:256], cb[:, 0:512], cb[:, 512:1024]

        def v(name, h):
            return vec[:, VEC.index(name), h:h + 1]

        def nv(name, h):
            return nvec[:, VEC.index(name), h:h + 1]

        xT2 = [sb(f"xT{i}", [128, NH, B, TT_ + 1]) for i in range(2)]
        hat = [sb(f"hat{i}", [128, HQ, 2, L]) for i in range(2)]
        KT = [sb(f"KT{i}", [128, NP, NH, 128]) for i in range(2)]
        VU = [sb(f"VU{i}", [128, NP, C]) for i in range(2)]
        AM = [sb(f"AM{i}", [128, NP, 256]) for i in range(2)]
        CT = [sb(f"CT{i}", [128, HQ]) for i in range(2)]
        bv = [sb(f"bv{i}", [128, NH, COLS]) for i in range(2)]
        gT = [sb(f"gT{i}", [128, NH, COLS]) for i in range(2)]

        bns = sb("bns", [128, NM, 6])
        mv = sb("mv", [128, NM, 2])
        rstd = sb("rstd", [128, NM])
        big = [sb(f"big{i}", [128, NH, COLS]) for i in range(6)]
        KSb = [sb(f"KS{i}", [128, QC, NJ * 2 * L]) for i in range(2)]
        KE = [sb(f"KE{i}", [128, QC, 2 * L]) for i in range(2)]
        qpad = [sb(f"qpad{i}", [128, QC, NJ, 2, 2, BL]) for i in range(2)]
        duo = [k[:, :, :].rearrange("p q n -> p (q n)").rearrange("p (a h n) -> p a h n", a=2, h=NH) for k in KSb]
        smalls = sb("smalls", [128, 2 * COLS])
        small, sml2 = smalls[:, 0:COLS], smalls[:, COLS:2 * COLS]
        FL = smalls[:, 0:25 * HQ].rearrange("p (q n) -> p q n", n=25)
        EF = sb("EF", [128, HQ, 25])
        hT = sb("hT", [128, NF, TT_])
        sg = sb("sg", [128, COLS])
        fsil = sb("fsil", [128, NM, C])
        TT = sb("TT", [128, NP * H, L])
        ST = sb("ST", [128, B, NH, N])
        rhs = sb("rhs", [128, 512])
        Y = sb("Y", [128, NM * H, N])
        AL = fsil[:, :, :].rearrange("p m c -> p (m c)").rearrange("p (s t) -> p s t", t=L)
        TL = Y[:, 0:8, :].rearrange("p g n -> p (g n)").rearrange("p (j t) -> p j t", t=L)
        prod = Y[:, 8:16, :].rearrange("p g n -> p (g n)")
        st1 = sb("st1", [128, NM * H])
        st2 = sb("st2", [128, NM * H])
        bank = [ps(f"bank{i}") for i in range(NB)]
        RY = ctx.enter_context(nc.psum_tensor("RY", [128, 2, 512], F32))
        PU, PS = ps("PU"), ps("PS")

        sems = {k: ctx.enter_context(nc.semaphore(f"s_{k}")) for k in ENG + DMAS}
        s_init = ctx.enter_context(nc.semaphore("s_init"))
        s_set = ctx.enter_context(nc.semaphore("s_set"))
        s_w = ctx.enter_context(nc.semaphore("s_w"))
        s_ffn = ctx.enter_context(nc.semaphore("s_ffn"))
        P = Progress(nc, sems)
        pe, act, dve, pool, sp = nc.tensor, nc.scalar, nc.vector, nc.gpsimd, nc.sync
        wait, done = P.wait, P.done

        am0 = duo[0][:, 0, 0, 0:256]
        stage = duo[1][:, 0].rearrange("p h n -> p (h n)")
        sp.dma_start(con[:, :], d["con"][:, 0:256]).then_inc(s_init, 16)
        sp.dma_start(am0, d["con"][:, 256:512]).then_inc(s_init, 16)
        sp.dma_start(stage, d["con"][:, 512:1536]).then_inc(s_init, 16)
        sp.dma_start(vec[:, :, :], d["vec"]).then_inc(s_init, 16)
        sp.dma_start(mask[:, :], d["mask"]).then_inc(s_init, 16)
        act.wait_ge(s_init, 80)
        act.dma_start(W[:, :], d["W"]).then_inc(s_w, 16)
        ints = [z[:, 0:NH * DH].bitcast(I32) for z in (VU[1][:, :, :].rearrange("p q c -> p (q c)"),
                                                       KT[1][:, :, :, :].rearrange("p q h k -> p (q h k)"),
                                                       hat[1][:, :, :, :].rearrange("p q x t -> p (q x t)"))]
        for t, name in zip(ints, ("w_gate", "w_up", "w_down")):
            act.dma_start(t, d[name]).then_inc(s_ffn, 16)
        setup = 0
        for value, col in ((LN_EPS, 0), (GN_EPS, 1), (1.0, 2), (0.0, 3)):
            dve.memset(eps[:, col:col + 1], value).then_inc(s_set, 1)
            setup += 1
        for t in (ST[:, :, :, :], xT2[1][:, :, :, TT_:TT_ + 1],
                  qpad[0][:, :, :, :, :, :], qpad[1][:, :, :, :, :, :]):
            dve.memset(t, 0.0).then_inc(s_set, 1)
            setup += 1
        for e in (pe, act, dve, pool):
            e.wait_ge(s_init, 80)
        dve.tensor_scalar(nvec[:, :, :], vec[:, :, :], -1.0, None, ALU.mult).then_inc(s_set, 1)
        dve.tensor_copy(cb[:, :], stage).then_inc(s_set, 1)
        for i in range(2):
            dve.tensor_copy(AM[i][:, :, :], am0.unsqueeze(1).to_broadcast([128, NP, 256])).then_inc(s_set, 1)
        setup += 4
        for e in (pe, act, dve, pool, sp):
            e.wait_ge(s_set, setup)

        ring = {"next": 0, "free": [None] * NB}

        def take():
            i = ring["next"]
            ring["next"] = (i + 1) % NB
            assert ring["free"][i] != "in use"
            wait("pe", ring["free"][i])
            ring["free"][i] = "in use"
            return i

        def project(i, weights, x, rows=128, base=0):
            for h in range(NH):
                m = pe.matmul(bank[i][base:base + rows, :], weights[:, h, :], x[:, h, :], start=(h == 0), stop=(h == NH - 1))
            return m

        x_in, x_out = d["x"], d["out"]

        marks = {}


        def norm(t, par, beside):
            xT, before = xT2[par], xT2[1 - par]
            X = smalls.rearrange("p (m c) -> p m c", m=NM)
            if "F" in beside or "ef" in marks:
                wait("sp", marks["ef"])
            for b in range(B):
                ld = done("xld", sp.dma_start(X[:, 2 * b:2 * b + 2, :],
                                              x_in[b, bass.ds(t * TT_, TT_), :].rearrange("(m p) c -> p m c", p=128)))
            yield
            wait("dve", ld)
            for m in range(NM):
                s = done("dve", dve.bn_stats(bns[:, m, :], X[:, m, :]))
            wait("dve", s)
            for m in range(NM):
                s = done("dve", dve.bn_aggr(mv[:, m, :], bns[:, m, :]))
            yield
            wait("act", s)
            a = done("act", act.activation(rstd[:, :], mv[:, :, 1], ACT.Ln, bias=eps[:, 0:1]))
            wait("act", a)
            a = done("act", act.activation(rstd[:, :], rstd[:, :], ACT.Exp, scale=-0.5))
            yield
            wait("dve", a)
            for m in range(NM):
                s = done("dve", dve.tensor_scalar(X[:, m, :], X[:, m, :], mv[:, m, 0:1], rstd[:, m:m + 1], ALU.subtract, ALU.mult))
            yield
            wait("pe", s)
            if "N" in beside or "xT free" in marks:
                wait("pool", marks["xT free"])
                wait("act", marks["xT free"])
            done("pool", pool.tensor_copy(xT[:, :, :, 0:1], before[:, :, :, TT_:TT_ + 1]))
            for h in range(NH):
                i = take()
                for m in range(NM):
                    q = pe.transpose(bank[i][:, 128 * m:128 * m + 128], X[:, m, 128 * h:128 * h + 128], ident)
                q = done("pe", q)
                wait("act", q)
                a = done("act", act.activation(xT[:, h, :, 1:TT_ + 1], bank[i][:, :].rearrange("p (b n) -> p b n", b=B), ACT.Copy))
                ring["free"][i] = a

        def front(par):
            (xx, xm, xwa, xk, kT, na) = big
            xv, xrg = duo[0][:, 0], duo[0][:, 1]
            tmp, vdf = duo[1][:, 0], duo[1][:, 1]
            xT = xT2[par]
            x_now = xT[:, :, :, 1:TT_ + 1]
            split = "p (b n) -> p b n"
            for h in range(NH):
                s = done("dve", dve.tensor_tensor(xx[:, h, :].rearrange(split, b=B), xT[:, h, :, 0:TT_], x_now[:, h], ALU.subtract))
            wait("dve", s)
            for h in range(NH):
                s = done("dve", dve.scalar_tensor_tensor(out=xm[:, h, :].rearrange(split, b=B), in0=xx[:, h, :].rearrange(split, b=B),
                                                         scalar=v("maa_x", h), in1=x_now[:, h], op0=ALU.mult, op1=ALU.add))
            yield
            i = take()
            wait("pe", s)
            q = done("pe", project(i, w1, xm))
            wait("act", q)
            a = done("act", act.activation(small[:, :], bank[i][:, :], ACT.Tanh))
            ring["free"][i] = a
            yield
            wait("pe", a)
            ready = {}
            tmps = (tmp, na)
            use = [None, None]
            for n, (f, dst, maa) in enumerate(((1, xwa, "maa_wa"), (2, xk, "maa_k"), (0, xrg, "maa_rg"), (3, xv, "maa_v"))):
                w = tmps[n % 2]
                for h in range(NH):
                    i = take()
                    q = done("pe", pe.matmul(bank[i][:, :], w2[32 * f:32 * f + 32, 128 * h:128 * h + 128],
                                             small[32 * f:32 * f + 32, :], start=True, stop=True))
                    wait("dve", q, use[n % 2])
                    s = done("dve", dve.scalar_tensor_tensor(out=w[:, h, :], in0=bank[i][:, :], scalar=v(maa, h),
                                                             in1=xx[:, h, :], op0=ALU.add, op1=ALU.mult))
                    ring["free"][i] = s
                    if h == 0:
                        yield
                    wait("pool", s)
                    g = done("pool", pool.tensor_tensor(dst[:, h, :].rearrange(split, b=B), w[:, h, :].rearrange(split, b=B),
                                                        x_now[:, h], ALU.add))
                use[n % 2] = g
                ready[f] = g
                yield
            i = take()
            wait("pe", ready[1])
            q = done("pe", project(i, wa1, xwa, rows=112))
            wait("act", q)
            a1 = done("act", act.activation(sml2[0:64, :], bank[i][0:64, :], ACT.Tanh))
            a = done("act", act.activation(sml2[64:112, :], bank[i][64:112, :], ACT.Copy))
            ring["free"][i] = a
            yield
            wait("pe", a)
            az, rz = xm, xx
            for h in range(NH):
                i = take()
                q = done("pe", pe.matmul(bank[i][:, :], wa2[0:64, 128 * h:128 * h + 128], sml2[0:64, :], start=True, stop=True))
                wait("act", q, ready[3])
                done("act", act.activation(az[:, h, :], bank[i][:, :], ACT.Abs, bias=v("decay", h)))
                a = done("act", act.activation(rz[:, h, :], bank[i][:, :], ACT.Relu, bias=nv("decay", h), scale=-1.0))
                ring["free"][i] = a
                yield
                i = take()
                q = done("pe", pe.matmul(bank[i][:, :], wa2[64:80, 128 * h:128 * h + 128], sml2[64:80, :], start=True, stop=True))
                wait("act", q, ready[3])
                a = done("act", act.activation(na[:, h, :], bank[i][:, :], ACT.Sigmoid, bias=nv("aaaaa", h), scale=-1.0))
                ring["free"][i] = a
            marks["z"] = a
            yield
            nma = xwa
            for h in range(NH):
                i = take()
                q = done("pe", pe.matmul(bank[i][:, :], wa2[96:112, 128 * h:128 * h + 128], sml2[96:112, :], start=True, stop=True))
                wait("act", q)
                a = done("act", act.activation(nma[:, h, :], bank[i][:, :], ACT.Sigmoid, bias=nv("misc_a", h), scale=-1.0))
                ring["free"][i] = a
            wait("pool", a)
            mix_a = nma
            nn = done("pool", pool.tensor_tensor(mix_a[:, :, :], na[:, :, :], nma[:, :, :], ALU.mult))
            yield
            wait("pe", ready[2])
            for h in range(NH):
                i = take()
                q = done("pe", project(i, wk[:, :, 128 * h:128 * h + 128], xk))
                wait("act", q)
                a = done("act", act.activation(kT[:, h, :], bank[i][:, :], ACT.Copy))
                ring["free"][i] = a
                yield
            k_ready = a
            i = take()
            q = done("pe", project(i, wk1, xk, rows=48))
            wait("act", q)
            done("act", act.activation(small[0:16, :], bank[i][0:16, :], ACT.Tanh))
            a = done("act", act.activation(small[32:48, :], bank[i][32:48, :], ACT.Copy))
            ring["free"][i] = a
            yield
            wait("pe", a)
            kk, mk = tmp, xk
            for h in range(NH):
                i = take()
                q = done("pe", pe.matmul(bank[i][:, :], wk2[0:16, 128 * h:128 * h + 128], small[0:16, :], start=True, stop=True))
                wait("dve", q, k_ready)
                s = done("dve", dve.tensor_tensor(kk[:, h, :], bank[i][:, :], kT[:, h, :], ALU.add))
                ring["free"][i] = s
                yield
                i = take()
                q = done("pe", pe.matmul(bank[i][:, :], wk2[32:48, 128 * h:128 * h + 128], small[32:48, :], start=True, stop=True))
                wait("act", q)
                a = done("act", act.activation(mk[:, h, :], bank[i][:, :], ACT.Sigmoid, bias=v("misc_k", h)))
                ring["free"][i] = a
            kk_ready, mk_ready = s, a
            yield
            sqk = rn = vdf
            wait("act", kk_ready)
            sq_ready = done("act", act.activation(sqk[:, :, :], kk[:, :, :], ACT.Square))
            yield
            wait("pe", ready[0])
            i = take()
            q = done("pe", project(i, g1, xrg))
            wait("act", q)
            a = done("act", act.activation(sml2[:, :], bank[i][:, :], ACT.Tanh))
            ring["free"][i] = a
            g_hidden = a
            yield
            wait("pe", sq_ready)
            for h in range(NH):
                i = take()
                q = done("pe", pe.matmul(bank[i][:, :], bd, sqk[:, h, :], start=True, stop=True))
                wait("dve", q)
                s = done("dve", dve.tensor_scalar(rn[:, h, :], bank[i][:, :], 1e-24, None, ALU.max))
                ring["free"][i] = s
            yield
            wait("act", s)
            a = done("act", act.activation(rn[:, :, :], rn[:, :, :], ACT.Ln))
            wait("act", a)
            a = done("act", act.activation(rn[:, :, :], rn[:, :, :], ACT.Exp, scale=-0.5))
            wait("pool", a)
            kk_fin = done("pool", pool.tensor_tensor(kk[:, :, :], kk[:, :, :], rn[:, :, :], ALU.mult))
            yield
            ii = []
            for h in range(NH):
                ii.append(take())
                q = done("pe", project(ii[h], wr[:, :, 128 * h:128 * h + 128], xrg))
                if h == 0:
                    yield
            rT = xrg
            wait("act", q)
            for h in range(NH):
                a = done("act", act.activation(rT[:, h, :], bank[ii[h]][:, :], ACT.Copy))
                ring["free"][ii[h]] = a
            r_ready = a
            yield
            wait("pe", ready[3])
            ii = []
            for h in range(NH):
                ii.append(take())
                q = done("pe", project(ii[h], wv[:, :, 128 * h:128 * h + 128], xv))
            marks["xv free"] = q
            for h in range(NH):
                vd = vdf.rearrange("p h n -> p (h n)").rearrange("p (q d t) -> p q d t", d=2, t=L)
                wait("act", q, kk_fin)
                done("act", act.activation(vd, bank[ii[h]][:, :].rearrange("p (q t) -> p q t", t=L).unsqueeze(2).to_broadcast([128, NQ, 2, L]), ACT.Copy))
                a = done("act", act.activation(bv[par][:, h, :], bank[ii[h]][:, :], ACT.Copy))
                ring["free"][ii[h]] = a
                yield
                wait("pe", a)
                for p4 in range(0, NP, 4):
                    i = take()
                    for n in range(4):
                        q = pe.transpose(bank[i][:, 128 * n:128 * n + 128], vd[:, 2 * (p4 + n):2 * (p4 + n) + 2].rearrange("p q d t -> p (q d t)"), ident)
                    q = done("pe", q)
                    wait("act", q)
                    ring["free"][i] = done("act", act.activation(VU[par][:, p4:p4 + 4, 128 * h:128 * h + 128],
                                                                 bank[i][:, :].rearrange("p (n c) -> p n c", n=4), ACT.Copy))
            v_ready, vd_read = a, q
            yield
            wait("pe", g_hidden)
            for h in range(NH):
                i = take()
                q = done("pe", pe.matmul(bank[i][:, :], g2[:, 128 * h:128 * h + 128], sml2[:, :], start=True, stop=True))
                wait("act", q)
                a = done("act", act.activation(gT[par][:, h, :], bank[i][:, :], ACT.Copy))
                ring["free"][i] = a
            marks["smalls free"] = q
            yield
            rz = xx
            wait("pool", marks["n"], mk_ready)
            n_read = g = done("pool", pool.tensor_tensor(mk[:, :, :], mk[:, :, :], rz[:, :, :], ALU.mult))
            wait("act", g)
            em_ready = done("act", act.activation(mk[:, :, :], mk[:, :, :], ACT.Exp, scale=-1.0))
            yield
            wait("dve", nn, k_ready)
            s = done("dve", dve.scalar_tensor_tensor(out=mix_a[:, :, :], in0=mix_a[:, :, :], scalar=1.0, in1=kT[:, :, :], op0=ALU.subtract, op1=ALU.mult))
            wait("dve", s, em_ready)
            k_fin = done("dve", dve.scalar_tensor_tensor(out=kT[:, :, :], in0=mix_a[:, :, :], scalar=-1.0, in1=mk[:, :, :], op0=ALU.mult, op1=ALU.mult))
            wait("dve", kk_fin)
            bneg = na
            b_fin = done("dve", dve.scalar_tensor_tensor(out=bneg[:, :, :], in0=na[:, :, :], scalar=1.0, in1=kk[:, :, :], op0=ALU.subtract, op1=ALU.mult))
            rk = vdf
            wait("dve", k_fin, r_ready, vd_read)
            for h in range(NH):
                s = done("dve", dve.scalar_tensor_tensor(out=rk[:, h, :], in0=rT[:, h, :], scalar=v("faaaa", h), in1=kT[:, h, :], op0=ALU.mult, op1=ALU.mult))
            yield
            wait("pe", s)
            for h in range(NH):
                i = take()
                q = done("pe", pe.matmul(bank[i][:, :], bd, rk[:, h, :], start=True, stop=True))
                wait("dve", q, v_ready)
                s = done("dve", dve.tensor_tensor(bv[par][:, h, :], bank[i][:, :], bv[par][:, h, :], ALU.mult))
                ring["free"][i] = s
            rk_free = q
            yield
            grp = "p h (g e) -> p (h g) e"
            cs, nd, cs_ready = xv, az, marks["cs"]
            csb = cs[:, :, :].rearrange(grp, e=BL)
            G = HQ * NJ
            dm, e2, e3 = mk, mix_a, xx
            dmb, e3b = (z[:, :, :].rearrange(grp, e=BL) for z in (dm, e3))
            wait("dve", k_fin, cs_ready)
            s1 = done("dve", dve.tensor_tensor(dmb, csb, csb[:, :, 3:4].to_broadcast([128, G, BL]), ALU.subtract))
            wait("dve", s1, k_fin)
            wait("pool", n_read, s1)
            g3 = done("pool", pool.tensor_tensor(e3b, csb[:, :, BL - 1:BL].to_broadcast([128, G, BL]), csb, ALU.subtract))
            s2 = done("dve", dve.tensor_tensor(e2[:, :, :], dm[:, :, :], nd[:, :, :], ALU.subtract))
            ef = marks["ef"]
            EFv = EF[:, :, :].rearrange("p q (i j) -> p q i j", i=5)
            wait("act", s2)
            xa = done("act", act.activation(e2[:, :, :], e2[:, :, :], ACT.Exp, scale=-1.0))
            ekey = nd
            wait("act", s2)
            xk_ = done("act", act.activation(ekey[:, :, :], dm[:, :, :], ACT.Exp))
            wait("act", xk_)
            xr = done("act", act.activation(dm[:, :, :], dm[:, :, :], ACT.Exp, scale=-1.0))
            wait("act", g3)
            xs = done("act", act.activation(e3[:, :, :], e3[:, :, :], ACT.Exp, scale=-1.0))
            yield
            wait("dve", xa)
            qa = done("dve", dve.tensor_tensor(e2[:, :, :], e2[:, :, :], kk[:, :, :], ALU.mult))
            wait("pool", xr)
            qr = done("pool", pool.tensor_tensor(dm[:, :, :], dm[:, :, :], rT[:, :, :], ALU.mult))
            five = "p h (q j e) -> p (h q) j e"
            a5, r5, kin, bin_, ek5, sf5 = (z[:, :, :].rearrange(five, j=NJ, e=BL) for z in (e2, dm, kT, bneg, ekey, e3))
            yield
            wait("dve", qr, qa, ef)
            hv = hat[par][:, :, :, :].rearrange("p q x (j e) -> p q x j e", e=BL)
            first = EFv[:, :, 0:NJ, 0:1].to_broadcast([128, HQ, NJ, BL])
            for x, own_q in ((0, a5), (1, r5)):
                s = done("dve", dve.tensor_tensor(hv[:, :, x], own_q, first, ALU.mult))
            done("dve", dve.tensor_copy(CT[par][:, :], EFv[:, :, NJ, 0]))
            wait("pool", qa, qr, ef, xk_, xs, b_fin, rk_free, s)
            wait("act", qa, qr)
            wait("dve", xk_, xs, k_fin, b_fin, rk_free)
            yield
            read = [None, None]
            made = {}

            def keys(qt):
                u = qt % 2
                qs = slice(QC * qt, QC * qt + QC)
                K, Q = KSb[u], qpad[u]
                wait("dve", read[u])
                wait("pool", read[u])
                wait("act", read[u])
                for hh in range(2):
                    p0 = 64 * hh
                    for x, own_q in ((0, a5), (1, r5)):
                        a = done("act", act.activation(Q[p0:p0 + 64, :, :, hh, x, :], own_q[p0:p0 + 64, qs], ACT.Copy))
                for x, z, who, eng in ((0, kin, "dve", dve), (1, bin_, "pool", pool)):
                    whole = K[:, :, :]
                    own = bass.AP(tensor=whole.tensor, offset=whole.offset + L * x,
                                  ap=[list(whole.ap[0]), [NJ * 2 * L, QC], [2 * L + BL, NJ], [1, BL]])
                    done(who, eng.tensor_tensor(own, z[:, qs], ek5[:, qs], ALU.mult))
                    wait(who, done(who, eng.tensor_tensor(z[:, qs], z[:, qs], sf5[:, qs], ALU.mult)))
                for i4 in range(1, NJ + 1):
                    fac = EFv[:, qs, i4, 1:i4 + 1].unsqueeze(3).to_broadcast([128, QC, i4, BL])
                    for x, z, who, eng in ((0, kin, "dve", dve), (1, bin_, "pool", pool)):
                        buf, at = (K, 2 * L * i4 + L * x) if i4 < NJ else (KE[u], L * x)
                        o = buf[:, :, at:at + BL * i4].rearrange("p q (j e) -> p q j e", e=BL)
                        m = done(who, eng.tensor_tensor(o, z[:, qs, 0:i4, :], fac, ALU.mult))
                        made[qt, x] = m
                made[qt, 2] = a

            def matrices(qt):
                h, b, u = qt // B, qt % B, qt % 2
                K, Q = KSb[u], qpad[u]
                wait("pe", *(made[qt, n] for n in range(3)))
                i = take()
                for n in range(QC // 2):
                    for cp in range(2):
                        o = bank[i][64 * cp:64 * cp + 64, 128 * n:128 * n + 128].rearrange("p (x e) -> p x e", e=L)
                        for j in range(NJ):
                            q = pe.matmul(o[:, :, BL * j:BL * j + BL], K[:, 2 * n + cp, 64 * j:64 * j + 64],
                                          Q[:, 2 * n + cp, j, :, :, :].rearrange("p a b e -> p (a b) e"), start=True, stop=True)
                q = done("pe", q)
                wait("dve", q)
                pairs = slice(4 * b, 4 * b + 4)
                am_ready = done("dve", dve.copy_predicated(AM[par][:, pairs, 128 * h:128 * h + 128],
                                                           mask[:, 0:128].unsqueeze(1).to_broadcast([128, 4, 128]),
                                                           bank[i][:, :].rearrange("p (n c) -> p n c", n=4)))
                ring["free"][i] = am_ready
                i = take()
                for n in range(QC // 2):
                    q = pe.transpose(bank[i][:, 128 * n:128 * n + 128], KE[u][:, 2 * n:2 * n + 2, :].rearrange("p q n -> p (q n)"), ident)
                read[u] = q = done("pe", q)
                wait("act", q)
                a = done("act", act.activation(KT[par][:, pairs, h, :], bank[i][:, :].rearrange("p (n c) -> p n c", n=4), ACT.Copy))
                ring["free"][i] = a
                return am_ready

            keys(0)
            yield
            for qt in range(NH * B):
                if qt + 1 < NH * B:
                    keys(qt + 1)
                    yield
                am_ready = matrices(qt)
                yield

        def decays(par):
            az, rz = big[1], big[0]
            wait("act", marks["z"])
            a = done("act", act.activation(az[:, :, :], az[:, :, :], ACT.Exp, scale=-1.0))
            wait("act", a)
            a = done("act", act.activation(az[:, :, :], az[:, :, :], ACT.Ln, bias=eps[:, 2:3]))
            yield
            wait("dve", a)
            s = done("dve", dve.scalar_tensor_tensor(out=rz[:, :, :], in0=az[:, :, :], scalar=0.5, in1=rz[:, :, :], op0=ALU.add, op1=ALU.add))
            wait("dve", s)
            nd = az
            marks["n"] = s
            s = done("dve", dve.tensor_scalar(nd[:, :, :], rz[:, :, :], MAXDECAY, None, ALU.min))
            yield
            cs = duo[0][:, 0]
            wait("dve", s, marks["xv free"])
            for h in range(NH):
                s = done("dve", dve.tensor_tensor_scan(cs[:, h, :], scanm, nd[:, h, :], 0.0, ALU.mult, ALU.add))
            marks["cs"] = s
            yield
            wait("pool", marks["smalls free"])
            zeroed = done("pool", pool.memset(FL[:, :, :], 0.0))
            wait("dve", zeroed, s)
            c4 = cs[:, :, :].rearrange("p h (q j e) -> p (h q) j e", j=NJ, e=BL)
            s = done("dve", dve.tensor_copy(FL[:, :, 0:24].rearrange("p q (a b) -> p q a b", b=6)[:, :, :, 0:1], c4[:, :, :, 3:4]))
            FLv = FL[:, :, :].rearrange("p q (i j) -> p q i j", i=5)
            for j in range(NJ - 1, -1, -1):
                wait("dve", s)
                s = done("dve", dve.tensor_tensor(FLv[:, :, j + 1:5, j:j + 1], FLv[:, :, j + 1:5, j + 1:j + 2],
                                                  c4[:, :, j, BL - 1:BL].unsqueeze(2).to_broadcast([128, HQ, 4 - j, 1]), ALU.add))
                if j == 2:
                    yield
            yield
            wait("act", s)
            marks["ef"] = done("act", act.activation(EF[:, :, :], FL[:, :, :], ACT.Exp, scale=-1.0))

        def ffn(par):
            s = last = None
            for b in range(B):
                x_now = xT2[par][:, :, b, 1:TT_ + 1]
                for n in range(0, NF, 2):
                    def hidden(w):
                        i = take()
                        for n2 in range(2):
                            for h in range(NH):
                                q = pe.matmul(bank[i][:, TT_ * n2:TT_ * n2 + TT_], w[:, h, 128 * (n + n2):128 * (n + n2) + 128],
                                              x_now[:, h], start=(h == 0), stop=(h == NH - 1))
                        return i, done("pe", q)

                    i, q = hidden(wg)
                    wait("act", q, s)
                    a = done("act", act.activation(sg[:, :], bank[i][:, :], ACT.Sigmoid))
                    wait("dve", a)
                    s = done("dve", dve.tensor_tensor(sg[:, :], sg[:, :], bank[i][:, :], ALU.mult))
                    ring["free"][i] = s
                    yield
                    i, q = hidden(wu)
                    wait("dve", s, q, last)
                    s = done("dve", dve.tensor_tensor(hT[:, n:n + 2, :], sg[:, :].rearrange("p (n c) -> p n c", n=2),
                                                      bank[i][:, :].rearrange("p (n c) -> p n c", n=2), ALU.mult))
                    ring["free"][i] = s
                    yield
                if b == B - 1:
                    marks["xT free"] = q
                wait("pe", s)
                i = take()
                for m in range(2):
                    for n in range(NF):
                        q = pe.matmul(bank[i][:, 256 * m:256 * m + 256], hT[:, n, 128 * m:128 * m + 128], wd[:, n, :],
                                      start=(n == 0), stop=(n == NF - 1))
                    if m == 0:
                        yield
                last = q = done("pe", q)
                wait("act", q, s)
                a = done("act", act.activation(sg[:, :], bank[i][:, :], ACT.Sigmoid))
                wait("dve", a, marks["inverted"])
                s = done("dve", dve.tensor_tensor(fsil[:, 2 * b:2 * b + 2, :], sg[:, :].rearrange("p (m c) -> p m c", m=2),
                                                  bank[i][:, :].rearrange("p (m c) -> p m c", m=2), ALU.mult))
                ring["free"][i] = s
                marks["ffn"] = s
                yield

        def convert():
            dve.wait_ge(s_ffn, 48)
            for t, w in zip(ints, (wg, wu, wd)):
                done("dve", dve.tensor_scalar(w[:, :, :].rearrange("p a b -> p (a b)"), t, 1.0 / 127.0, None, ALU.mult))
                yield

        def back(t, par, other):
            for cp in range(2):
                for p in range(0, NP, 4):
                    src = AM[par][64 * cp + 32:64 * cp + 64, p:p + 4, :].rearrange("s p (h x t) -> s (p h) x t", h=H, x=2)
                    w = done("awr", sp.dma_start(d["scrA"][cp, :, p:p + 4].rearrange("s p h t -> s (p h) t"), src[:, :, 0, :]))
            wait("sp", w)
            for jh in range(2):
                for cp in range(2):
                    l0 = 64 * jh + 32 * cp
                    w = done("ard", sp.dma_start(AL[l0:l0 + 32, :, :], d["scrA"][cp].rearrange("s p h t -> (p h) s t")))
            yield
            s = done("dve", dve.tensor_copy(TL[:, :, :], ti.rearrange("p (j t) -> p j t", t=L)))
            wait("dve", w)
            for tt in range(1, L):
                nj = tt // 2 + 1
                pv = prod[:, 0:nj * (tt + 1)].rearrange("p (j s) -> p j s", s=tt + 1)
                wait("dve", s)
                s = done("dve", dve.tensor_tensor(pv, TL[:, 0:nj, 0:tt + 1],
                                                  AL[:, 0:tt + 1, tt].unsqueeze(1).to_broadcast([128, nj, tt + 1]), ALU.mult))
                wait("dve", s)
                s = done("dve", dve.tensor_reduce(TL[:, 0:nj, tt:tt + 1], pv, AX.X, ALU.add))
                if tt % 3 == 0:
                    yield
            marks["inverted"] = s
            wait("sp", s)
            w = done("twr", sp.dma_start(d["scrT"], TL[:, :, :]))
            wait("sp", w)
            for cp in range(2):
                for jh in range(2):
                    p0, l0 = 64 * cp, 64 * jh + 32 * cp
                    w = done("trd", sp.dma_start(TT[p0 + jh:p0 + L:2, :, :], d["scrT"][l0:l0 + 32].rearrange("l j t -> j l t")))
            yield
            wait("pe", w)
            A, V = AM[par], VU[par]
            y_read = [None, None]
            upd = None
            rhs_free = None
            u_read = None
            av = {}

            def values(c):
                p0 = 64 * (c % 2)
                wait("pe", y_read[c % 2])
                for b in range(B):
                    pr = b * (NP // B) + c // 2
                    for h in range(H):
                        q = pe.matmul(RY[p0:p0 + 64, h % 2, 128 * b + 64 * (h // 2):128 * b + 64 * (h // 2) + 64],
                                      A[p0:p0 + 32, pr, 64 * h:64 * h + 64], V[p0:p0 + 32, pr, 64 * h:64 * h + 64],
                                      start=(b == 0 and h < 2), stop=True, skip_group_check=True)
                av[c] = done("pe", q)

            values(0)
            for c in range(NQ // B):
                cp = c % 2
                p0 = 64 * cp
                if upd:
                    yield
                wait("pe", av[c], upd)
                for h in range(H):
                    h2, hh = h // 2, h % 2
                    for b in range(B):
                        q = pe.matmul(RY[p0:p0 + 64, hh, 128 * b + 64 * h2:128 * b + 64 * h2 + 64],
                                      hat[par][64 * hh:64 * hh + 64, h2 * NQ + b * QC + c, :, :].rearrange("p x t -> p (x t)"),
                                      ST[64 * hh:64 * hh + 64, b, h2, :], start=False, stop=False, skip_group_check=True)
                q = done("pe", q)
                wait("act", q, rhs_free)
                a = done("act", act.activation(rhs[p0:p0 + 32, :].rearrange("p (x n) -> p x n", x=2), RY[p0:p0 + 32, :, 0:256], ACT.Copy))
                yield
                wait("pe", a, u_read)
                for b in range(B):
                    pr = b * (NP // B) + c // 2
                    for h in range(H):
                        q = pe.matmul(PU[p0 + 32:p0 + 64, 256 * b + 64 * h:256 * b + 64 * h + 64], TT[p0:p0 + 32, pr * H + h, :],
                                      rhs[p0:p0 + 32, 256 * (h % 2) + 128 * b + 64 * (h // 2):256 * (h % 2) + 128 * b + 64 * (h // 2) + 64],
                                      start=True, stop=True)
                q = done("pe", q)
                rhs_free = q
                wait("dve", q)
                vu = V[:, :, :].rearrange("p (b n) c -> p b n c", b=B)
                u_read = done("dve", dve.tensor_copy(vu[p0 + 32:p0 + 64, :, c // 2, :], PU[p0 + 32:p0 + 64, :].rearrange("p (b c) -> p b c", b=B)))
                yield
                if c + 1 < QC:
                    values(c + 1)
                    yield
                wait("pe", u_read)
                for b in range(B):
                    pr = b * (NP // B) + c // 2
                    for h in range(H):
                        h2, hh = h // 2, 64 * (h % 2)
                        q = pe.matmul(PS[hh:hh + 64, 128 * b + 64 * h2:128 * b + 64 * h2 + 64], KT[par][p0:p0 + 64, pr, h2, hh:hh + 64],
                                      V[p0:p0 + 64, pr, 64 * h:64 * h + 64], start=True, stop=True)
                q = done("pe", q)
                wait("dve", q)
                for b in range(B):
                    for h2 in range(NH):
                        k = h2 * NQ + b * (NQ // B) + c
                        upd = done("dve", dve.scalar_tensor_tensor(
                            out=ST[:, b, h2, :], in0=ST[:, b, h2, :], scalar=CT[par][:, k:k + 1],
                            in1=PS[:, 128 * b + 64 * h2:128 * b + 64 * h2 + 64], op0=ALU.mult, op1=ALU.add))
                yield
                for b in range(B):
                    pr = b * (NP // B) + c // 2
                    for h in range(H):
                        q = pe.matmul(RY[p0 + 32:p0 + 64, h % 2, 128 * b + 64 * (h // 2):128 * b + 64 * (h // 2) + 64], 
                                      A[p0 + 32:p0 + 64, pr, 64 * h + 32:64 * h + 64], V[p0 + 32:p0 + 64, pr, 64 * h:64 * h + 64],
                                      start=False, stop=True, skip_group_check=True)
                q = done("pe", q)
                wait("act", q)
                r0 = 32 * (c % 4)
                yv = Y[:, :, :].rearrange("p (b m g x) n -> p b m g x n", b=B, m=NM // B, x=2)
                for x in range(2):
                    y_read[cp] = done("act", act.activation(yv[r0:r0 + 32, :, c // 4, :, x, :], RY[p0 + 32:p0 + 64, x, 0:256]
                                                            .rearrange("p (b g n) -> p b g n", b=B, g=NH), ACT.Copy))
                yield
            spare = hat[par][:, :, :, :].rearrange("p q x t -> p (q x t)")
            yb = spare[:, 0:NH * COLS].rearrange("p (h n) -> p h n", h=NH)
            sq = spare[:, NH * COLS:].rearrange("p (g n) -> p g n", n=N)
            wait("dve", y_read[0], y_read[1])
            G = NM * H
            s = done("dve", dve.tensor_reduce(st1[:, :].unsqueeze(2), Y[:, :, :], AX.X, ALU.add))
            wait("dve", s)
            s = done("dve", dve.scalar_tensor_tensor(out=Y[:, :, :], in0=st1[:, :].unsqueeze(2).to_broadcast([128, G, N]), scalar=-1.0 / N,
                                                     in1=Y[:, :, :], op0=ALU.mult, op1=ALU.add))
            wait("act", s)
            a = done("act", act.activation(sq, Y[:, :, :], ACT.Square))
            wait("dve", a)
            s = done("dve", dve.tensor_reduce(st2[:, :].unsqueeze(2), sq, AX.X, ALU.add))
            wait("act", s)
            a = done("act", act.activation(st2[:, :], st2[:, :], ACT.Ln, bias=eps[:, 1:2], scale=1.0 / N))
            wait("act", a)
            a = done("act", act.activation(st2[:, :], st2[:, :], ACT.Exp, scale=-0.5))
            wait("dve", a)
            g = done("dve", dve.tensor_tensor(Y[:, :, :], Y[:, :, :], st2[:, :].unsqueeze(2).to_broadcast([128, G, N]), ALU.mult))
            yield
            wait("pe", g)
            ym = Y[:, :, :].rearrange("p (m h) n -> p m (h n)", h=H)
            for h in range(NH):
                i = take()
                for m in range(NM):
                    q = pe.transpose(bank[i][:, 128 * m:128 * m + 128], ym[:, m, 128 * h:128 * h + 128], ident)
                q = done("pe", q)
                wait("dve", q)
                s = done("dve", dve.scalar_tensor_tensor(out=yb[:, h, :], in0=bank[i][:, :], scalar=v("ln_w", h),
                                                         in1=bv[par][:, h, :], op0=ALU.mult, op1=ALU.add))
                ring["free"][i] = s
                wait("dve", s)
                g = done("dve", dve.scalar_tensor_tensor(out=yb[:, h, :], in0=yb[:, h, :], scalar=v("ln_b", h),
                                                         in1=gT[par][:, h, :], op0=ALU.add, op1=ALU.mult))
            wait("sp", q)
            for b in range(B):
                x2 = done("xre", sp.dma_start(ym[:, 2 * b:2 * b + 2, :], x_in[b, bass.ds(t * TT_, TT_), :].rearrange("(m p) c -> p m c", p=128)))
            yield
            for _ in other:
                yield
            wait("pe", g)
            for m2 in range(NM // 2):
                i = take()
                for n2 in range(2):
                    m = 2 * m2 + n2
                    for h in range(NH):
                        q = pe.matmul(bank[i][:, 256 * n2:256 * n2 + 256], yb[:, h, 128 * m:128 * m + 128], wo[:, h, :],
                                      start=(h == 0), stop=(h == NH - 1))
                q = done("pe", q)
                wait("dve", q, marks["ffn"])
                fs, xo = fsil[:, 2 * m2:2 * m2 + 2, :], ym[:, 2 * m2:2 * m2 + 2, :]
                s = done("dve", dve.tensor_tensor(fs, fs, bank[i][:, :].rearrange("p (m c) -> p m c", m=2), ALU.mult))
                ring["free"][i] = s
                wait("dve", s, x2)
                s = done("dve", dve.tensor_tensor(fs, fs, xo, ALU.add))
                wait("act", s)
                done("ost", act.dma_start(x_out[m2, bass.ds(t * TT_, TT_), :].rearrange("(m p) c -> p m c", p=128), fs))
                yield

        def step(stream):
            for _ in stream:
                return True
            return False

        def run(streams):
            for name in ORDER:
                if name in streams and not step(streams[name]):
                    del streams[name]
            assert not streams

        def section(norm_of=None, front_of=None, back_of=None):
            P.section()
            ring["free"] = [None] * NB
            marks.clear()
            streams = {}
            if front_of:
                streams["F"], streams["D"] = front(front_of[1]), decays(front_of[1])
            if back_of:
                streams["N"] = ffn(back_of[1])
                streams["B"] = back(*back_of, streams["N"])
            elif front_of:
                streams["N"] = convert()
            if norm_of:
                streams["L"] = norm(*norm_of, streams)
            run(streams)
            P.end()

        section(norm_of=(0, 0))
        pe.wait_ge(s_w, 16)
        section(norm_of=(1, 1), front_of=(0, 0))
        with nc.Fori(0, NT // 2 - 1) as i:
            section(norm_of=(2 * i + 2, 0), front_of=(2 * i + 1, 1), back_of=(2 * i, 0))
            section(norm_of=(2 * i + 3, 1), front_of=(2 * i + 2, 0), back_of=(2 * i + 1, 1))
        section(front_of=(NT - 1, 1), back_of=(NT - 2, 0))
        section(back_of=(NT - 1, 1))

def pack(inputs, np):
    g = {k.removeprefix("L0_attn_").removeprefix("L0_ffn_"): np.asarray(a) for k, a in inputs.items()}
    W = np.zeros((128, WTOT), np.float32)

    def put(name, a, at=0, rows=0):
        lo = WCOL[name][0] + at
        W[rows:rows + a.shape[0], lo:lo + a.shape[1]] = a

    def halves(name, a, width=None, at=0):
        w = width or a.shape[1]
        for h in range(2):
            put(name, a[128 * h:128 * h + 128], at=h * w + at)

    halves("w1", g["time_maa_w1"])
    put("w2", g["time_maa_w2"].reshape(128, 256))
    for n, s in (("wr", "w_receptance"), ("wk", "w_key"), ("wv", "w_value"), ("wo", "w_output")):
        halves(n, g[s].T)
    for s, at in (("time_decay_w1", 0), ("time_aaa_w1", 64), ("ma_w1", 96)):
        halves("wa1", g[s], 112, at)
    for s, at in (("time_kkk_w1", 0), ("mk_w1", 32)):
        halves("wk1", g[s], 48, at)
    put("wa2", g["time_decay_w2"])
    put("wa2", g["time_aaa_w2"], rows=64)
    put("wa2", g["ma_w2"], rows=96)
    put("wk2", g["time_kkk_w2"])
    put("wk2", g["mk_w2"], rows=32)
    halves("g1", g["gate_w1"])
    put("g2", g["gate_w2"])
    names = {"maa_x": "time_maa_x", "maa_rg": "time_maa_rg", "maa_wa": "time_maa_wa", "maa_k": "time_maa_k", "maa_v": "time_maa_v",
             "decay": "time_decay", "aaaaa": "time_aaaaa", "misc_a": "time_misc_a", "misc_k": "time_misc_k", "faaaa": "time_faaaa"}
    vec = np.stack([g[names.get(n, n)].reshape(2, 128).T for n in VEC], axis=1)
    con = np.zeros((128, CTOT), np.float32)

    def const(name):
        a, b = CCOL[name]
        return con[:, a:b]

    mask = np.zeros((128, 128), np.uint32)
    p = np.arange(128)
    const("ident")[p, p] = 1
    const("bd")[:, :] = p[:, None] // 64 == p[None, :] // 64
    const("scan")[:, :] = np.arange(512)[None, :] % BL != 0
    key, s = p % 64 // 32, p % 32
    col = np.arange(256)
    xq, tq = col % 64 // 32, col % 32
    mask[:, :] = np.where(xq[None, :] == 0, s[:, None] < tq[None, :], s[:, None] <= tq[None, :])[:, 0:128]
    const("am0")[:, :] = (key[:, None] == 1) & (xq[None, :] == 0) & (s[:, None] == tq[None, :])
    j, t = np.arange(512) // 32, np.arange(512) % 32
    const("ti")[:, :] = p[:, None] // 64 + 2 * j[None, :] == t[None, :]

    def fold(a):
        return np.ascontiguousarray(a.reshape(a.shape[0] // 128, 128, a.shape[1]).transpose(1, 0, 2).reshape(128, -1))

    return {"x": np.ascontiguousarray(g["x"]), "W": W, "vec": np.ascontiguousarray(vec), "con": con, "mask": mask,
            "w_gate": fold(g["w_gate"].T), "w_up": fold(g["w_up"].T), "w_down": fold(g["w_down"].T)}


def build(bacc, arrays):
    nc = bacc.Bacc("TRN2", target_bir_lowering=False, num_devices=1)
    d = {k: nc.dram_tensor(f"in_{k}", list(a.shape), mybir.dt.from_np(a.dtype), kind="ExternalInput").ap() for k, a in arrays.items()}
    d["out"] = nc.dram_tensor("out_0", [B, T, C], F32, kind="ExternalOutput").ap()
    d["scrA"] = nc.dram_tensor("scrA", [2, L, NP, H, L], F32, kind="Internal").ap()
    d["scrT"] = nc.dram_tensor("scrT", [NLANE, 16, L], F32, kind="Internal").ap()
    program(nc, d)
    return nc


def kernel(**inputs):
    import numpy as _np
    import concourse.bacc as _bacc
    from concourse.bass_utils import run_bass_kernel_spmd as _run

    arrays = pack(inputs, _np)
    nc = build(_bacc, arrays)
    r = _run(nc, [{f"in_{k}": a for k, a in arrays.items()}], core_ids=[0])
    return r.results[0]["out_0"]
```
